# Optimizing a Trainium2 kernel written in Bass

```python
import numpy as np
import jax
import jax.numpy as jnp

def _softmax(x, axis=-1):
    return jax.nn.softmax(x, axis=axis)

def _gelu(x):
    return jax.nn.gelu(x, approximate=True)

def _silu(x):
    return jax.nn.silu(x)

def _sigmoid(x):
    return jax.nn.sigmoid(x)

def _layernorm(x, axis=-1, eps=1e-05):
    m = jnp.mean(x, axis=axis, keepdims=True)
    v = jnp.var(x, axis=axis, keepdims=True)
    return (x - m) / jnp.sqrt(v + eps)

def _scatter_add(tgt, idx, src, axis=0):
    return tgt.at[idx].add(src)

def _segment_sum(src, seg, n):
    return jax.ops.segment_sum(src, seg, n)
kernel_name = 'mk_gnn_resnorm_d4_gnn_r64_c63165'

def setup_inputs(seed: int=0):
    np.random.seed(seed)
    _w = jnp.asarray

    def _rec_inputs():
        import jax
        import jax.numpy as jnp
        _gk = jax.random.key(seed)
        x = -0.000202 + 1 * jax.random.normal(jax.random.fold_in(_gk, 1), (50000, 128), jnp.float32)
        src = jax.random.randint(jax.random.fold_in(_gk, 2), (12500,), 0, 50000, jnp.int32)
        dst = jax.random.randint(jax.random.fold_in(_gk, 3), (12500,), 0, 50000, jnp.int32)
        _o = jnp.argsort(dst, stable=True)
        src = src[_o]
        dst = dst[_o]
        edge_attr_128 = -5.16925e-05 + 1.00005 * jax.random.normal(jax.random.fold_in(_gk, 12), (12500, 128), jnp.float32)
        edge_attr_20 = -8.62073e-06 + 0.999901 * jax.random.normal(jax.random.fold_in(_gk, 13), (12500, 20), jnp.float32)
        edge_weight = jax.random.uniform(jax.random.fold_in(_gk, 15), (12500,), jnp.float32, 0.0, 0.999999)
        return (x, src, dst, edge_attr_128, edge_attr_20, edge_weight)
    x, src, dst, edge_attr_128, edge_attr_20, edge_weight = _rec_inputs()

    def _L0_gnn_setup():
        import jax, jax.numpy as jnp
        import numpy as np
        N, E, H = (50000, 12500, 128)
        EPS = 1e-07
        BN_EPS = 1e-05
        LN_EPS = 1e-05
        key = jax.random.key(seed)
        ks = jax.random.split(key, 12)
        return dict(h=jax.random.normal(ks[0], (N, H), jnp.float32), edge_index=jax.random.randint(ks[1], (2, E), 0, N, dtype=jnp.int32), edge_attr=jax.random.normal(ks[2], (E, H), jnp.float32), bn_weight=1.0 + 0.1 * jax.random.normal(ks[3], (H,), jnp.float32), bn_bias=0.1 * jax.random.normal(ks[4], (H,), jnp.float32), bn_mean=0.1 * jax.random.normal(ks[5], (H,), jnp.float32), bn_var=jax.random.uniform(ks[6], (H,), jnp.float32, 0.5, 1.5), t=jnp.array(1.0, jnp.float32), W1=jax.random.normal(ks[7], (H, 2 * H), jnp.float32) / np.float32(np.sqrt(H)), b1=jnp.zeros((2 * H,), jnp.float32), ln_weight=jnp.ones((2 * H,), jnp.float32), ln_bias=jnp.zeros((2 * H,), jnp.float32), W2=jax.random.normal(ks[8], (2 * H, H), jnp.float32) / np.float32(np.sqrt(2 * H)), b2=jnp.zeros((H,), jnp.float32))
    _L0_gnn_all = _L0_gnn_setup()
    _L0_gnn_in = {k: v for k, v in _L0_gnn_all.items() if k in ('bn_weight', 'bn_bias', 'bn_mean', 'bn_var', 't', 'W1', 'b1', 'ln_weight', 'ln_bias', 'W2', 'b2')}
    del _L0_gnn_all

    def _L1_gnn_setup():
        import jax, jax.numpy as jnp
        import numpy as np
        N = 50000
        E = 9375
        D = 128
        BN_EPS = 1e-05
        GIN_EPS = 0.0
        key = jax.random.key(seed)
        ks = jax.random.split(key, 8)
        x = jax.random.normal(ks[0], (N, D), dtype=jnp.float32)
        edge_index = jax.random.randint(ks[1], (2, E), 0, N, dtype=jnp.int64)
        s = 1.0 / np.sqrt(D)
        w1 = jax.random.uniform(ks[2], (D, D), jnp.float32, -s, s)
        b1 = jax.random.uniform(ks[3], (D,), jnp.float32, -s, s)
        w2 = jax.random.uniform(ks[4], (D, D), jnp.float32, -s, s)
        b2 = jax.random.uniform(ks[5], (D,), jnp.float32, -s, s)
        gamma = jnp.ones((D,), jnp.float32)
        beta = jnp.zeros((D,), jnp.float32)
        return {'x': x, 'edge_index': edge_index, 'w1': w1, 'b1': b1, 'w2': w2, 'b2': b2, 'gamma': gamma, 'beta': beta}
    _L1_gnn_all = _L1_gnn_setup()
    _L1_gnn_in = {k: v for k, v in _L1_gnn_all.items() if k in ('w1', 'b1', 'w2', 'b2', 'gamma', 'beta')}
    del _L1_gnn_all

    def _L2_gnn_setup():
        import jax, jax.numpy as jnp
        import numpy as np
        N_ATOMS = 50000
        N_EDGES = 25000
        NAB = 128
        NRBF = 20
        NF = 128
        LOG2 = float(np.log(2.0))

        def shifted_softplus(x):
            return jax.nn.softplus(x) - LOG2
        key = jax.random.key(seed)
        ks = jax.random.split(key, 16)
        x = jax.random.normal(ks[0], (N_ATOMS, NAB), dtype=jnp.float32)
        f_ij = jax.random.normal(ks[1], (N_EDGES, NRBF), dtype=jnp.float32)
        rcut_ij = jax.random.uniform(ks[2], (N_EDGES,), dtype=jnp.float32)
        idx_i = jnp.sort(jax.random.randint(ks[3], (N_EDGES,), 0, N_ATOMS))
        idx_j = jax.random.randint(ks[4], (N_EDGES,), 0, N_ATOMS)

        def xavier(k, shape):
            fan_in, fan_out = shape
            s = float(np.sqrt(6.0 / (fan_in + fan_out)))
            return jax.random.uniform(k, shape, dtype=jnp.float32, minval=-s, maxval=s)
        W_in2f = xavier(ks[5], (NAB, NF))
        W_f1 = xavier(ks[6], (NRBF, NF))
        b_f1 = jnp.zeros((NF,), jnp.float32)
        W_f2 = xavier(ks[7], (NF, NF))
        b_f2 = jnp.zeros((NF,), jnp.float32)
        W_o1 = xavier(ks[8], (NF, NAB))
        b_o1 = jnp.zeros((NAB,), jnp.float32)
        W_o2 = xavier(ks[9], (NAB, NAB))
        b_o2 = jnp.zeros((NAB,), jnp.float32)
        return {'x': x, 'f_ij': f_ij, 'rcut_ij': rcut_ij, 'idx_i': idx_i, 'idx_j': idx_j, 'W_in2f': W_in2f, 'W_f1': W_f1, 'b_f1': b_f1, 'W_f2': W_f2, 'b_f2': b_f2, 'W_o1': W_o1, 'b_o1': b_o1, 'W_o2': W_o2, 'b_o2': b_o2}
    _L2_gnn_all = _L2_gnn_setup()
    _L2_gnn_in = {k: v for k, v in _L2_gnn_all.items() if k in ('W_in2f', 'W_f1', 'b_f1', 'W_f2', 'b_f2', 'W_o1', 'b_o1', 'W_o2', 'b_o2')}
    del _L2_gnn_all

    def _L3_gnn_setup():
        import jax, jax.numpy as jnp
        import numpy as np
        N, E = (50000, 25000)
        D_IN, D_HID, D_OUT = (128, 128, 128)

        def _sage_conv(x, src, dst, Wl, bl, Wr):
            n = x.shape[0]
            agg = jax.ops.segment_sum(x[src], dst, num_segments=n)
            cnt = jax.ops.segment_sum(jnp.ones_like(dst, dtype=x.dtype), dst, num_segments=n)
            mean = agg / jnp.maximum(cnt, 1.0)[:, None]
            return mean @ Wl.T + bl + x @ Wr.T
        key = jax.random.key(seed)
        ks = jax.random.split(key, 8)
        x = jax.random.normal(ks[0], (N, D_IN), dtype=jnp.float32)
        edge_index = jax.random.randint(ks[1], (2, E), 0, N, dtype=jnp.int64)

        def lin(k, fan_out, fan_in):
            bound = 1.0 / np.sqrt(fan_in)
            return jax.random.uniform(k, (fan_out, fan_in), minval=-bound, maxval=bound, dtype=jnp.float32)
        W1l = lin(ks[2], D_HID, D_IN)
        b1l = jnp.zeros((D_HID,), dtype=jnp.float32)
        W1r = lin(ks[3], D_HID, D_IN)
        W2l = lin(ks[4], D_OUT, D_HID)
        b2l = jnp.zeros((D_OUT,), dtype=jnp.float32)
        W2r = lin(ks[5], D_OUT, D_HID)
        return {'x': x, 'edge_index': edge_index, 'W1l': W1l, 'b1l': b1l, 'W1r': W1r, 'W2l': W2l, 'b2l': b2l, 'W2r': W2r}
    _L3_gnn_all = _L3_gnn_setup()
    _L3_gnn_in = {k: v for k, v in _L3_gnn_all.items() if k in ('W1l', 'b1l', 'W1r', 'W2l', 'b2l', 'W2r')}
    del _L3_gnn_all
    return {'x': x, 'src': src, 'dst': dst, 'edge_attr_128': edge_attr_128, 'edge_attr_20': edge_attr_20, 'edge_weight': edge_weight, 'L0_gnn_bn_weight': _L0_gnn_in['bn_weight'], 'L0_gnn_bn_bias': _L0_gnn_in['bn_bias'], 'L0_gnn_bn_mean': _L0_gnn_in['bn_mean'], 'L0_gnn_bn_var': _L0_gnn_in['bn_var'], 'L0_gnn_t': _L0_gnn_in['t'], 'L0_gnn_W1': _L0_gnn_in['W1'], 'L0_gnn_b1': _L0_gnn_in['b1'], 'L0_gnn_ln_weight': _L0_gnn_in['ln_weight'], 'L0_gnn_ln_bias': _L0_gnn_in['ln_bias'], 'L0_gnn_W2': _L0_gnn_in['W2'], 'L0_gnn_b2': _L0_gnn_in['b2'], 'L1_gnn_w1': _L1_gnn_in['w1'], 'L1_gnn_b1': _L1_gnn_in['b1'], 'L1_gnn_w2': _L1_gnn_in['w2'], 'L1_gnn_b2': _L1_gnn_in['b2'], 'L1_gnn_gamma': _L1_gnn_in['gamma'], 'L1_gnn_beta': _L1_gnn_in['beta'], 'L2_gnn_W_in2f': _L2_gnn_in['W_in2f'], 'L2_gnn_W_f1': _L2_gnn_in['W_f1'], 'L2_gnn_b_f1': _L2_gnn_in['b_f1'], 'L2_gnn_W_f2': _L2_gnn_in['W_f2'], 'L2_gnn_b_f2': _L2_gnn_in['b_f2'], 'L2_gnn_W_o1': _L2_gnn_in['W_o1'], 'L2_gnn_b_o1': _L2_gnn_in['b_o1'], 'L2_gnn_W_o2': _L2_gnn_in['W_o2'], 'L2_gnn_b_o2': _L2_gnn_in['b_o2'], 'L3_gnn_W1l': _L3_gnn_in['W1l'], 'L3_gnn_b1l': _L3_gnn_in['b1l'], 'L3_gnn_W1r': _L3_gnn_in['W1r'], 'L3_gnn_W2l': _L3_gnn_in['W2l'], 'L3_gnn_b2l': _L3_gnn_in['b2l'], 'L3_gnn_W2r': _L3_gnn_in['W2r']}

def reference(x, src, dst, edge_attr_128, edge_attr_20, edge_weight, L0_gnn_bn_weight, L0_gnn_bn_bias, L0_gnn_bn_mean, L0_gnn_bn_var, L0_gnn_t, L0_gnn_W1, L0_gnn_b1, L0_gnn_ln_weight, L0_gnn_ln_bias, L0_gnn_W2, L0_gnn_b2, L1_gnn_w1, L1_gnn_b1, L1_gnn_w2, L1_gnn_b2, L1_gnn_gamma, L1_gnn_beta, L2_gnn_W_in2f, L2_gnn_W_f1, L2_gnn_b_f1, L2_gnn_W_f2, L2_gnn_b_f2, L2_gnn_W_o1, L2_gnn_b_o1, L2_gnn_W_o2, L2_gnn_b_o2, L3_gnn_W1l, L3_gnn_b1l, L3_gnn_W1r, L3_gnn_W2l, L3_gnn_b2l, L3_gnn_W2r):
    import jax
    import jax.numpy as jnp

    def _L0_gnn_ref(h, edge_index, edge_attr, bn_weight, bn_bias, bn_mean, bn_var, t, W1, b1, ln_weight, ln_bias, W2, b2):
        import jax, jax.numpy as jnp
        import numpy as np
        N, E, H = (50000, 12500, 128)
        EPS = 1e-07
        BN_EPS = 1e-05
        LN_EPS = 1e-05
        x = h
        hn = (x - bn_mean) * jax.lax.rsqrt(bn_var + BN_EPS) * bn_weight + bn_bias
        hn = jax.nn.relu(hn)
        src, dst = (edge_index[0], edge_index[1])
        msg = jax.nn.relu(hn[src] + edge_attr) + EPS
        logits = msg * t
        seg_max = jax.ops.segment_max(jax.lax.stop_gradient(logits), dst, num_segments=N)
        seg_max = jnp.where(jnp.isfinite(seg_max), seg_max, 0.0)
        ex = jnp.exp(logits - seg_max[dst])
        denom = jax.ops.segment_sum(ex, dst, num_segments=N)
        alpha = ex / (denom[dst] + 1e-16)
        agg = jax.ops.segment_sum(msg * alpha, dst, num_segments=N)
        out = agg + hn
        y = out @ W1 + b1
        mu = y.mean(-1, keepdims=True)
        var = ((y - mu) ** 2).mean(-1, keepdims=True)
        y = (y - mu) * jax.lax.rsqrt(var + LN_EPS) * ln_weight + ln_bias
        y = jax.nn.relu(y)
        y = y @ W2 + b2
        return x + y

    def _L1_gnn_ref(x, edge_index, w1, b1, w2, b2, gamma, beta):
        import jax, jax.numpy as jnp
        import numpy as np
        N = 50000
        E = 9375
        D = 128
        BN_EPS = 1e-05
        GIN_EPS = 0.0
        src, dst = (edge_index[0], edge_index[1])
        agg = jax.ops.segment_sum(x[src], dst, num_segments=N)
        h = (1.0 + GIN_EPS) * x + agg
        h = jax.nn.relu(h @ w1 + b1)
        h = h @ w2 + b2
        mean = jnp.mean(h, axis=0)
        var = jnp.var(h, axis=0)
        h = (h - mean) * jax.lax.rsqrt(var + BN_EPS) * gamma + beta
        h = jax.nn.relu(h)
        return x + h

    def _L2_gnn_ref(x, f_ij, rcut_ij, idx_i, idx_j, W_in2f, W_f1, b_f1, W_f2, b_f2, W_o1, b_o1, W_o2, b_o2):
        import jax, jax.numpy as jnp
        import numpy as np
        N_ATOMS = 50000
        N_EDGES = 25000
        NAB = 128
        NRBF = 20
        NF = 128
        LOG2 = float(np.log(2.0))

        def shifted_softplus(x):
            return jax.nn.softplus(x) - LOG2
        h = x @ W_in2f
        Wij = shifted_softplus(f_ij @ W_f1 + b_f1) @ W_f2 + b_f2
        Wij = Wij * rcut_ij[:, None]
        x_ij = h[idx_j] * Wij
        y = jax.ops.segment_sum(x_ij, idx_i, num_segments=N_ATOMS)
        out = shifted_softplus(y @ W_o1 + b_o1) @ W_o2 + b_o2
        return out

    def _L3_gnn_ref(x, edge_index, W1l, b1l, W1r, W2l, b2l, W2r):
        import jax, jax.numpy as jnp
        import numpy as np
        N, E = (50000, 25000)
        D_IN, D_HID, D_OUT = (128, 128, 128)

        def _sage_conv(x, src, dst, Wl, bl, Wr):
            n = x.shape[0]
            agg = jax.ops.segment_sum(x[src], dst, num_segments=n)
            cnt = jax.ops.segment_sum(jnp.ones_like(dst, dtype=x.dtype), dst, num_segments=n)
            mean = agg / jnp.maximum(cnt, 1.0)[:, None]
            return mean @ Wl.T + bl + x @ Wr.T
        src, dst = (edge_index[0], edge_index[1])
        h = jax.nn.relu(_sage_conv(x, src, dst, W1l, b1l, W1r))
        return _sage_conv(h, src, dst, W2l, b2l, W2r)
    edge_index = jnp.stack([src, dst])
    x = _layernorm(x + _L0_gnn_ref(x, edge_index, edge_attr_128, L0_gnn_bn_weight, L0_gnn_bn_bias, L0_gnn_bn_mean, L0_gnn_bn_var, L0_gnn_t, L0_gnn_W1, L0_gnn_b1, L0_gnn_ln_weight, L0_gnn_ln_bias, L0_gnn_W2, L0_gnn_b2), axis=-1)
    x = _layernorm(x + _L1_gnn_ref(x, edge_index, L1_gnn_w1, L1_gnn_b1, L1_gnn_w2, L1_gnn_b2, L1_gnn_gamma, L1_gnn_beta), axis=-1)
    x = _layernorm(x + _L2_gnn_ref(x, edge_attr_20, edge_weight, src, dst, L2_gnn_W_in2f, L2_gnn_W_f1, L2_gnn_b_f1, L2_gnn_W_f2, L2_gnn_b_f2, L2_gnn_W_o1, L2_gnn_b_o1, L2_gnn_W_o2, L2_gnn_b_o2), axis=-1)
    x = _layernorm(x + _L3_gnn_ref(x, edge_index, L3_gnn_W1l, L3_gnn_b1l, L3_gnn_W1r, L3_gnn_W2l, L3_gnn_b2l, L3_gnn_W2r), axis=-1)
    return x

_drawn_inputs = setup_inputs


def setup_inputs(seed=0):
    import zlib

    import numpy as np

    out = dict(_drawn_inputs(seed))
    spreads = {'L0_gnn_b1': (0.0, 0.1),
     'L0_gnn_ln_weight': (1.0, 0.2),
     'L0_gnn_ln_bias': (0.0, 0.1),
     'L0_gnn_b2': (0.0, 0.1),
     'L1_gnn_gamma': (1.0, 0.2),
     'L1_gnn_beta': (0.0, 0.1),
     'L2_gnn_b_f1': (0.0, 0.8),
     'L2_gnn_b_f2': (0.0, 0.56),
     'L2_gnn_b_o1': (0.0, 0.1),
     'L2_gnn_b_o2': (0.0, 0.1),
     'L3_gnn_b1l': (0.0, 0.1),
     'L3_gnn_b2l': (0.0, 0.1)}
    factors = {'L1_gnn_b2': 8.0}
    for name, (base, spread) in spreads.items():
        noise = np.random.default_rng([zlib.crc32(name.encode()), seed]).standard_normal(out[name].shape)
        drawn = base * np.exp(spread * noise) if base else spread * noise
        out[name] = jnp.asarray(drawn.astype(out[name].dtype))
    for name, factor in factors.items():
        out[name] = (out[name] * factor).astype(out[name].dtype)
    return out
```

```python
import concourse.bass as bass
import numpy as np
from concourse import mybir
from contextlib import ExitStack

F32, BF16, I32 = mybir.dt.float32, mybir.dt.bfloat16, mybir.dt.int32
ALU, ACT, AX = mybir.AluOpType, mybir.ActivationFunctionType, mybir.AxisListType
N, E, D, RBF = 50000, 12500, 128, 20
P, R = 125, 4
G = P * R
NG, EG = N // G, E // G
SPLIT = 112
U = 4
EPS = 1e-5
NOWHERE = 100000


class At:

    def __init__(self, k, c):
        self.k, self.c = k, c
        self.slot = c % U

    @property
    def n(self):
        return self.k * U + self.c if not isinstance(self.k, int) else self.c

    @property
    def turn(self):
        return self.k + self.c // U

    def fixed(self):
        return isinstance(self.k, int)


def wait(eng, sem, at, per=1, late=0, base=0):
    if at.fixed():
        if at.c - late >= 0:
            eng.wait_ge(sem, base + (at.c - late + 1) * per)
    else:
        eng.wait_ge(sem, at.k * (U * per) + (base + (at.c - late + 1) * per))


def wait_slot(eng, sems, at, per=16, late=0):
    c = at.c - late
    if at.fixed():
        if c >= 0:
            eng.wait_ge(sems[c % U], (c // U + 1) * per)
    else:
        eng.wait_ge(sems[c % U], at.k * per + (c // U + 1) * per)


def run(eng, groups, stages):
    lag = max(s[0] for s in stages)
    first = -(-(lag + U) // U) * U
    last = max(first, groups // U * U)

    def step(k, c, lo):
        for late, stage in stages:
            if lo or 0 <= c - late < groups:
                stage(At(k, c - late))

    for i in range(min(first, groups + lag)):
        step(0, i, False)
    if last > first:
        with eng.Fori(first // U, last // U) as k:
            for c in range(U):
                step(k, c, True)
    for i in range(last, groups + lag):
        step(0, i, False)


def rows(table, at, base=0):
    ap = table[bass.ds(at.n * G + base, G), :] if not at.fixed() else table[at.n * G + base:at.n * G + base + G, :]
    return ap.rearrange("(p r) d -> p (r d)", p=P)


def move(eng, out, in_, sem):
    eng.dma_start(out[0:SPLIT], in_[0:SPLIT]).then_inc(sem, 16)
    eng.dma_start(out[SPLIT:P], in_[SPLIT:P]).then_inc(sem, 16)


class Kit:

    def __init__(self, nc):
        self.nc, self.taken = nc, []

    def sem(self, name):
        self.taken.append(self.nc.alloc_semaphore(name=name))
        return self.taken[-1]

    def end_phase(self):
        self.nc.clear_and_free_semaphores(self.taken)
        self.nc.all_engine_barrier()
        self.taken = []


def sem_list(K, name, n=U):
    return [K.sem(f"{name}{i}") for i in range(n)]


def setup(nc, K, I, ctx):
    def keep(name, shape, dt=F32):
        return K.ctx.enter_context(nc.sbuf_tensor(name, shape, dt))

    def tmp(name, shape, dt=F32):
        return ctx.enter_context(nc.sbuf_tensor(name, shape, dt))

    def sem(name):
        return K.sem(name)

    K.ident = keep("ident", [128, 128])
    K.eps = keep("eps", [128, 1])
    K.one = keep("one", [128, 1])
    K.bn_sum, K.fold, K.bs, K.bo = keep("bn_sum", [128, 2]), keep("fold", [128, 8]), keep("bs", [128, 1]), keep("bo", [128, 1])
    K.spc, K.alone, K.bo2_rows = keep("spc", [128, 128]), keep("alone", [128, 128]), keep("bo2_rows", [128, 128])
    K.ones3 = keep("ones3", [3, 128], BF16)
    COLS = ["bn_weight", "bn_bias", "bn_mean", "bn_var", "g0", "g1", "c0", "c1", "L1_b1", "L1_b2", "gamma",
            "beta", "bf1", "bf2", "bo1", "bo2", "b1l", "t", "s0", "o0", "L2_c", "tmp", "ssp0"]
    K.col = {n: i for i, n in enumerate(COLS)}
    K.cols = keep("cols", [128, len(COLS)])
    K.W1c = keep("W1c", [128, 256])
    K.W2 = keep("W2", [128, 2, 128])
    K.w = keep("w", [128, 11, 128])
    K.wi = {n: i for i, n in enumerate(["w1", "w2", "in2f", "f2", "o1", "o2", "W1lT", "W1rT", "W2lT", "W2rT", "cW"])}
    K.wf1 = keep("wf1", [RBF, 128])
    K.bias = keep("bias", [3, 640], BF16)
    K.same = keep("same", [128, E + 1], BF16)
    K.src = keep("src", [P, EG, R], I32)
    K.from_ = keep("from_", [P, EG, R], I32)
    K.first = keep("first_", [P, EG, R], I32)
    K.of_h3 = keep("of_h3", [P, EG, R], I32)
    K.to_s = keep("to_s", [P, EG, R], I32)
    K.to_d = keep("to_d", [P, EG, R], I32)
    dst = K.dst = keep("dst", [P, EG, R], I32)
    K.slot = keep("d_slot", [P, EG, R], I32)
    raw = tmp("raw", [128, 4, 128])
    brow = tmp("brow", [1, 640])
    bpart = tmp("bpart", [1, 3, 640], BF16)
    brest = tmp("brest", [1, 2, 640])
    mean = tmp("mean_w", [128, 2])
    dT = tmp("dT", [128, E // 5 + 1], I32)
    nxt = tmp("nxt", [P, EG, R], I32)
    fl = tmp("fl", [P, EG, R])
    fl2 = tmp("fl2", [P, EG, R])
    node = tmp("node", [P, N // P], I32)
    last = tmp("lastv", [1, 1], I32)

    loaded, padded, parts_in, consts, made = sem("loaded"), sem("padded"), sem("parts_in"), sem("consts"), sem("made")
    shifted, flags, node_made, map_init = sem("shifted"), sem("flags"), sem("node_made"), sem("map_init")
    sq, tposed, parts, dloaded, dused, idx_made = sem("sq"), sem("tposed"), sem("parts"), sem("dloaded"), sem("dused"), sem("idx_made")
    lasts = sem("lasts")
    CH = E // 5
    vecs = [("bn_weight", "L0_gnn_bn_weight"), ("bn_bias", "L0_gnn_bn_bias"), ("bn_mean", "L0_gnn_bn_mean"),
            ("bn_var", "L0_gnn_bn_var"), ("L1_b1", "L1_gnn_b1"), ("L1_b2", "L1_gnn_b2"), ("gamma", "L1_gnn_gamma"),
            ("beta", "L1_gnn_beta"), ("bf1", "L2_gnn_b_f1"), ("bf2", "L2_gnn_b_f2"), ("bo1", "L2_gnn_b_o1"),
            ("bo2", "L2_gnn_b_o2"), ("b1l", "L3_gnn_b1l")]
    K.c = lambda n: K.cols[:, K.col[n]:K.col[n] + 1]
    K.W = lambda n: K.w[:, K.wi[n], :]
    loads = [(K.c(n), I[k].rearrange("(p o) -> p o", o=1)) for n, k in vecs]
    for n, k in (("g", "L0_gnn_ln_weight"), ("c", "L0_gnn_ln_bias")):
        for h in range(2):
            loads.append((K.c(f"{n}{h}"), I[k][128 * h:128 * h + 128].rearrange("(p o) -> p o", o=1)))
    loads.append((K.bo2_rows[:, :], I["L2_gnn_b_o2"].rearrange("(a n) -> a n", a=1).to_broadcast([128, 128])))
    loads.append((K.c("t"), I["L0_gnn_t"].rearrange("(a o) -> a o", o=1).to_broadcast([128, 1])))
    loads += [(K.W1c[:, :], I["L0_gnn_W1"]), (K.W2[:, :, :], I["L0_gnn_W2"].rearrange("(h p) n -> p h n", h=2)),
              (K.W("w1"), I["L1_gnn_w1"]), (K.W("w2"), I["L1_gnn_w2"]), (K.W("in2f"), I["L2_gnn_W_in2f"]),
              (K.W("f2"), I["L2_gnn_W_f2"]), (K.W("o1"), I["L2_gnn_W_o1"]), (K.W("o2"), I["L2_gnn_W_o2"]),
              (K.wf1[:, :], I["L2_gnn_W_f1"]), (brow[:, 0:256], I["L0_gnn_b1"].rearrange("(a n) -> a n", a=1)),
              (brow[:, 256:384], I["L0_gnn_b2"].rearrange("(a n) -> a n", a=1)),
              (brow[:, 384:512], I["L3_gnn_b2l"].rearrange("(a n) -> a n", a=1)),
              (brow[:, 512:640], I["L2_gnn_b_o2"].rearrange("(a n) -> a n", a=1)),
              (K.src[:, :, :], I["src"].rearrange("(g p r) -> p g r", p=P, r=R)),
              (dst[:, :, :], I["dst"].rearrange("(g p r) -> p g r", p=P, r=R))]
    for i, k in enumerate(["L3_gnn_W1l", "L3_gnn_W1r", "L3_gnn_W2l", "L3_gnn_W2r"]):
        loads.append((raw[:, i, :], I[k]))
    pad = K.dst_pad

    with nc.Block() as block:
        @block.sync
        def _(sp):
            for out, in_ in loads:
                sp.dma_start(out, in_, allow_slow_non_contiguous=True).then_inc(loaded, 16)
            sp.wait_ge(lasts, 1)
            sp.dma_start(pad[0:1, :], last[:, :]).then_inc(padded, 16)
            sp.dma_start(pad[E + 1:E + 2, :], last[:, :]).then_inc(padded, 16)
            sp.dma_start(pad[1:E + 1, :], I["dst"].rearrange("(e o) -> e o", o=1)).then_inc(padded, 16)
            sp.wait_ge(padded, 48)
            sp.dma_start(nxt[:, :, :], pad[2:E + 2, :].rearrange("(g p r) o -> p g (r o)", p=P, r=R)).then_inc(shifted, 16)
            for i in range(5):
                if i:
                    sp.wait_ge(dused, i)
                sp.dma_start(dT[:, :], pad[CH * i:CH * i + CH + 1, :].rearrange("e o -> o e").to_broadcast([128, CH + 1])).then_inc(dloaded, 16)
            sp.wait_ge(parts, 1)
            for i in range(3):
                sp.dma_start(K.bias[i:i + 1, :], bpart[:, i, :]).then_inc(parts_in, 16)
            sp.wait_ge(parts_in, 48)

        @block.scalar
        def _(act):
            act.wait_ge(node_made, 1)
            act.dma_start(K.M.rearrange("(p n) o -> p (n o)", p=P), node[:, :]).then_inc(map_init, 16)
            act.wait_ge(map_init, 16)
            act.wait_ge(loaded, 16 * len(loads))
            act.wait_ge(consts, 2)
            nc.scalar.activation(K.c("tmp"), K.c("bn_var"), ACT.Sqrt, bias=K.eps[:, 0:1]).then_inc(sq, 1)

        @block.gpsimd
        def _(pool):
            nc.gpsimd.iota(node[:, :], pattern=[[1, N // P]], base=0, channel_multiplier=N // P).then_inc(node_made, 1)
            nc.gpsimd.iota(K.slot[:, :, :], pattern=[[G, EG], [1, R]], base=N, channel_multiplier=R).then_inc(idx_made, 1)
            nc.gpsimd.memset(K.ident[:, :], 0.0).then_inc(consts, 1)
            nc.gpsimd.memset(K.eps[:, :], EPS).then_inc(consts, 1)
            pool.wait_ge(consts, 2)
            nc.gpsimd.affine_select(out=K.ident[:, :], in_=K.ident[:, :], compare_op=ALU.not_equal, fill=1.0, base=0,
                                    pattern=[[-1, 128]], channel_multiplier=1).then_inc(consts, 1)
        @block.vector
        def _(dve):
            chain = [0]

            def link(ins):
                chain[0] += 1
                ins.then_inc(made, 1)
                dve.wait_ge(made, chain[0])

            nc.vector.memset(last[:, :], -1).then_inc(lasts, 1)
            nc.vector.memset(K.ones3[:, :], 1.0)
            nc.vector.memset(K.one[:, :], 1.0)
            dve.wait_ge(loaded, 16 * len(loads))
            dve.wait_ge(shifted, 16)
            nc.vector.tensor_tensor(fl[:, :, :], dst[:, :, :], nxt[:, :, :], ALU.is_equal).then_inc(flags, 1)
            dve.wait_ge(flags, 1)
            nc.vector.tensor_scalar(fl2[:, :, :], fl[:, :, :], float(NOWHERE), None, ALU.mult).then_inc(flags, 1)
            dve.wait_ge(flags, 2)
            nc.vector.tensor_tensor(K.to_d[:, :, :], dst[:, :, :], fl2[:, :, :], ALU.add).then_inc(flags, 1)
            for i in range(5):
                dve.wait_ge(dloaded, 16 * (i + 1))
                nc.vector.tensor_tensor(K.same[:, CH * i:CH * i + CH], dT[:, 0:CH], dT[:, 1:CH + 1], ALU.is_equal).then_inc(dused, 1)
            link(nc.vector.memset(K.same[:, E:E + 1], 0.0))
            link(nc.vector.reduce_sum(mean[:, 0:1], K.W1c[:, :], AX.X))
            link(nc.vector.tensor_scalar(mean[:, 1:2], mean[:, 0:1], 1.0 / 256, None, ALU.mult))
            link(nc.vector.tensor_scalar(K.W1c[:, :], K.W1c[:, :], mean[:, 1:2], None, ALU.subtract))
            link(nc.vector.reduce_sum(mean[0:1, 0:1], brow[:, 0:256], AX.X))
            link(nc.vector.tensor_scalar(mean[0:1, 1:2], mean[0:1, 0:1], 1.0 / 256, None, ALU.mult))
            link(nc.vector.tensor_scalar(brow[:, 0:256], brow[:, 0:256], mean[0:1, 1:2], None, ALU.subtract))
            link(nc.vector.tensor_copy(bpart[:, 0, :], brow[:, :]))
            link(nc.vector.tensor_tensor(brest[:, 0, :], brow[:, :], bpart[:, 0, :], ALU.subtract))
            link(nc.vector.tensor_copy(bpart[:, 1, :], brest[:, 0, :]))
            link(nc.vector.tensor_tensor(brest[:, 1, :], brest[:, 0, :], bpart[:, 1, :], ALU.subtract))
            nc.vector.tensor_copy(bpart[:, 2, :], brest[:, 1, :]).then_inc(parts, 1)
            dve.wait_ge(sq, 1)
            link(nc.vector.reciprocal(K.c("s0"), K.c("tmp")))
            link(nc.vector.tensor_tensor(K.c("s0"), K.c("s0"), K.c("bn_weight"), ALU.mult))
            link(nc.vector.tensor_tensor(K.c("o0"), K.c("s0"), K.c("bn_mean"), ALU.mult))
            link(nc.vector.tensor_tensor(K.c("o0"), K.c("bn_bias"), K.c("o0"), ALU.subtract))
            dve.wait_ge(tposed, 1)
            link(nc.vector.tensor_copy(K.w[:, 6:10, :], K.ps[0][:, :].rearrange("p (a b) -> p a b", a=4)))

        @block.tensor
        def _(pe):
            pe.wait_ge(loaded, 16 * len(loads))
            pe.wait_ge(consts, 3)
            for i in range(4):
                last_t = nc.tensor.transpose(K.ps[0][:, 128 * i:128 * i + 128], raw[:, i, :], K.ident[:, :])
            last_t.then_inc(tposed, 1)


def scatter_rows(nc, pool, table, idx, data, sem, limit):
    for g in range(EG):
        for r in range(R):
            pool.indirect_dma_start(out=table, out_offset=bass.IndirectOffsetOnAxis(ap=idx[:, g, r:r + 1], axis=0),
                                    in_=data(g, r), in_offset=None, bounds_check=limit,
                                    oob_is_err=False).then_inc(sem, 16)


def gather_rows(nc, pool, data, table, idx, sem, before=lambda g: None):
    for g in range(EG):
        before(g)
        for r in range(R):
            pool.indirect_dma_start(out=data(g, r), out_offset=None, in_=table,
                                    in_offset=bass.IndirectOffsetOnAxis(ap=idx[:, g, r:r + 1], axis=0)).then_inc(sem(g), 16)


def gen_dense(nc, K, name, groups, x_in, out, out_base, agg, side=None, clear=None):
    ctx = ExitStack()

    def sb(n, shape, dt=F32):
        return ctx.enter_context(nc.sbuf_tensor(f"{name}_{n}", shape, dt))

    def sem(n):
        return K.sem(f"{name}_{n}")

    with ctx:
        X = [sb(f"x{i}", [P, R, D]) for i in range(U)]
        HT = [sb(f"hT{i}", [128, R * P]) for i in range(2)]
        SQ = [sb(f"sq{i}", [P, R, 256], BF16) for i in range(2)]
        SS = [sb(f"ss{i}", [P, R]) for i in range(2)]
        Z = [sb(f"z{i}", [P, R, 256]) for i in range(2)]
        ZT = [sb(f"zT{i}", [128, 2, R * P]) for i in range(2)]
        O = [sb(f"o{i}", [P, R, D]) for i in range(2)]
        X1 = [sb(f"x1{i}", [P, R, D]) for i in range(U)]
        norm = Norm(nc, K, name, ctx)
        pT, pY, pZ, pO = K.ps[0], K.ps[1:3], K.ps[3:5], K.ps[5]
        x_in_s, stored = sem_list(K, f"{name}_xin"), sem_list(K, f"{name}_stored")
        xT, h, y, ssq, std, rstd, z, zT, zr, o, res = [sem(n) for n in
            ("xT", "h", "y", "ssq", "std", "rstd", "z", "zT", "zr", "o", "res")]
        spread = Spread(nc, K, name, ctx, agg) if agg is not None else None
        ha = sem("ha") if agg is not None else h

        zero = sb("zero", [P, R * D]) if clear is not None else None
        cleared, zeroed = (sem("cleared"), sem("zeroed")) if clear is not None else (None, None)

        with nc.Block() as block:
            if side is not None:
                block.gpsimd(side)

            @block.sync
            def _(sp):
                def load(at):
                    wait(sp, res, at, late=U)
                    move(sp, X[at.slot][:, :, :].rearrange("p r d -> p (r d)"), x_in(at), x_in_s[at.slot])

                def store(at):
                    wait(sp, norm.done, at)
                    move(sp, rows(out, at, out_base), X1[at.slot][:, :, :].rearrange("p r d -> p (r d)"), stored[at.slot])

                def clear_acc(at):
                    move(sp, rows(clear, at), zero[:, :], cleared)

                stages = [(0, load), (3, store)]
                if clear is not None:
                    sp.wait_ge(zeroed, 1)
                    stages.append((3, clear_acc))
                run(sp, groups, stages)
                if clear is not None:
                    sp.dma_start(clear[N:N + P, :], zero[:, 0:D]).then_inc(cleared, 16)
                    sp.wait_ge(cleared, 32 * groups + 16)
                for i in range(U):
                    sp.wait_ge(stored[i], 32 * ((groups - i + U - 1) // U))

            @block.tensor
            def _(pe):
                def transpose_z(at):
                    wait(pe, z, at)
                    wait(pe, zr, at, late=1)
                    for j in range(R):
                        for hf in range(2):
                            t = nc.tensor.transpose(pZ[hf][:, P * j:P * j + P], Z[at.slot % 2][:, j, 128 * hf:128 * hf + 128],
                                                    K.ident[0:P, 0:P])
                    t.then_inc(zT, 1)

                def first(at):
                    wait(pe, ha, at)
                    wait(pe, z, at, late=1)
                    for j in range(R):
                        out_ = pY[j // 2][0:P, 256 * (j % 2):256 * (j % 2) + 256]
                        nc.tensor.matmul(out_, HT[at.slot % 2][:, P * j:P * j + P], K.W1c[:, :], start=True, stop=False)
                        t = nc.tensor.matmul(out_, K.ones3[:, 0:P], K.bias[:, 0:256], start=False, stop=True)
                    t.then_inc(y, 1)

                def transpose_x(at):
                    wait_slot(pe, x_in_s, at, per=32)
                    wait(pe, h, at, late=1)
                    for j in range(R):
                        t = nc.tensor.transpose(pT[:, P * j:P * j + P], X[at.slot][:, j, :], K.ident[0:P, 0:P])
                    t.then_inc(xT, 1)

                def second(at):
                    wait(pe, zr, at)
                    wait(pe, res, at, late=1)
                    for j in range(R):
                        out_ = pO[0:P, D * j:D * j + D]
                        for hf in range(2):
                            nc.tensor.matmul(out_, ZT[at.slot % 2][:, hf, P * j:P * j + P], K.W2[:, hf, :], start=hf == 0, stop=False)
                        t = nc.tensor.matmul(out_, K.ones3[:, 0:P], K.bias[:, 256:384], start=False, stop=True)
                    t.then_inc(o, 1)

                run(pe, groups, [(3, transpose_z), (2, first), (1, transpose_x), (3, second)])

            @block.scalar
            def _(act):
                def relu_z(at):
                    wait(act, zT, at)
                    wait(act, o, at, late=2)
                    for hf in range(2):
                        t = nc.scalar.activation(ZT[at.slot % 2][:, hf, :], pZ[hf][:, 0:R * P], ACT.Relu,
                                                 bias=K.c(f"c{hf}"), scale=K.c(f"g{hf}"))
                    t.then_inc(zr, 1)

                def squares(at):
                    wait(act, y, at)
                    wait(act, rstd, at, late=2)
                    for j in range(R):
                        t = nc.scalar.activation(SQ[at.slot % 2][:, j, :], pY[j // 2][0:P, 256 * (j % 2):256 * (j % 2) + 256], ACT.Square,
                                                 accum_out=SS[at.slot % 2][:, j:j + 1])
                    t.then_inc(ssq, 1)
                    wait(act, ssq, at)
                    nc.scalar.activation(SS[at.slot % 2][:, :], SS[at.slot % 2][:, :], ACT.Sqrt, bias=K.eps[0:P, :],
                                         scale=1.0 / 256).then_inc(std, 1)

                def hidden(at):
                    wait(act, xT, at)
                    wait(act, y, at, late=2)
                    nc.scalar.activation(HT[at.slot % 2][:, :], pT[:, 0:R * P], ACT.Relu, bias=K.c("o0"),
                                         scale=K.c("s0")).then_inc(h, 1)

                run(act, groups, [(3, relu_z), (2, squares), (4, norm.std_of(act)), (1, hidden)])

            @block.vector
            def _(dve):
                def add_agg(at):
                    a = spread.scan(dve, at, ha)
                    wait(dve, h, at)
                    T = HT[at.slot % 2][:, :].rearrange("f (r p) -> f r p", r=R)
                    nc.vector.tensor_tensor(T, T, by_row(a[:, :]), ALU.add).then_inc(ha, 1)

                def scale(at):
                    wait(dve, std, at)
                    wait(dve, z, at, late=1)
                    nc.vector.reciprocal(SS[at.slot % 2][:, :], SS[at.slot % 2][:, :]).then_inc(rstd, 1)
                    wait(dve, rstd, at)
                    wait(dve, zT, at, late=2)
                    for j in range(R):
                        t = nc.vector.tensor_scalar(Z[at.slot % 2][:, j, :], pY[j // 2][0:P, 256 * (j % 2):256 * (j % 2) + 256],
                                                    SS[at.slot % 2][:, j:j + 1], None, ALU.mult)
                    t.then_inc(z, 1)

                def residual(at):
                    wait(dve, o, at)
                    wait(dve, norm.done, at, late=2)
                    nc.vector.scalar_tensor_tensor(out=O[at.slot % 2][:, :, :], in0=X[at.slot][:, :, :], scalar=2.0,
                                                   in1=pO[0:P, :].rearrange("p (r d) -> p r d", r=R), op0=ALU.mult,
                                                   op1=ALU.add).then_inc(res, 1)

                def finish(at):
                    wait_slot(dve, stored, at, per=32, late=U)
                    norm.apply(dve, at, O[at.slot % 2], X1[at.slot])

                if clear is not None:
                    nc.vector.memset(zero[:, :], 0.0).then_inc(zeroed, 1)
                stages = [(2, scale), (3, residual), (3, norm.stats_of(dve, O, res)), (4, finish)]
                if agg is not None:
                    stages.insert(1, (1, add_agg))
                run(dve, groups, stages)


class Norm:

    def __init__(self, nc, K, name, ctx):
        self.nc, self.K = nc, K
        self.st = [ctx.enter_context(nc.sbuf_tensor(f"{name}_st{i}", [P, R, 6], F32)) for i in range(2)]
        self.mv = [ctx.enter_context(nc.sbuf_tensor(f"{name}_mv{i}", [P, R, 2], F32)) for i in range(2)]
        self.sd = [ctx.enter_context(nc.sbuf_tensor(f"{name}_sd{i}", [P, R], F32)) for i in range(2)]
        self.tick = ctx.enter_context(nc.sbuf_tensor(f"{name}_tick", [1, 2], F32))
        self.stats, self.moments, self.std, self.rstd, self.done = [
            K.sem(f"{name}_ln_{n}") for n in ("stats", "moments", "std", "rstd", "done")]

    def stats_of(self, dve, rows_, ready):
        def stage(at):
            i = at.slot % 2
            wait(dve, ready, at)
            for j in range(R):
                t = self.nc.vector.bn_stats(self.st[i][:, j, :], rows_[i][:, j, :])
            t.then_inc(self.stats, 1)
            wait(dve, self.stats, at)
            wait(dve, self.done, at, late=2)
            self.nc.vector.memset(self.tick[:, i:i + 1], 0.0)
            for j in range(R):
                t = self.nc.vector.bn_aggr(self.mv[i][:, j, :], self.st[i][:, j, :])
            t.then_inc(self.moments, 1)
        return stage

    def std_of(self, act):
        def stage(at):
            i = at.slot % 2
            wait(act, self.moments, at)
            wait(act, self.done, at, late=2)
            self.nc.scalar.activation(self.sd[i][:, :], self.mv[i][:, :, 1], ACT.Sqrt, bias=self.K.eps[0:P, :]).then_inc(self.std, 1)
        return stage

    def apply(self, dve, at, rows_, out):
        i = at.slot % 2
        wait(dve, self.std, at)
        self.nc.vector.reciprocal(self.sd[i][:, :], self.sd[i][:, :]).then_inc(self.rstd, 1)
        wait(dve, self.rstd, at)
        for j in range(R):
            t = self.nc.vector.tensor_scalar(out[:, j, :], rows_[:, j, :], self.mv[i][:, j, 0:1], self.sd[i][:, j:j + 1],
                                             ALU.subtract, ALU.mult)
        t.then_inc(self.done, 1)


def cut(big, n, fixed, shift=0):
    return big[:, n * G + shift:n * G + G + shift] if fixed else big[:, bass.ds(n * G + shift, G)]


def backward(at):
    return EG - 1 - at.n if at.fixed() else at.k * -U + (EG - 1 - at.c)


def by_row(tile):
    return tile.rearrange("f (p r) -> f r p", r=R)


def tiles(tile):
    return tile.rearrange("f (r p) -> f r p", r=R)


def softmax_heads(nc, K, QH, MX):
    ctx = ExitStack()
    with ctx:
        def sb(n, shape, dt=F32, k=2):
            return [ctx.enter_context(nc.sbuf_tensor(f"sm_{n}{i}", shape, dt)) for i in range(k)]

        def sem(n):
            return K.sem(f"sm_{n}")

        X, A = sb("x", [P, R * D], k=U), sb("a", [P, R * D], k=U)
        HN, M2, PEN = sb("hn", [128, G]), sb("m2", [128, G]), sb("pen", [128, G])
        pX, pA = K.ps[0:2], K.ps[2:4]
        loaded = sem_list(K, "sm_loaded")
        xT, hn, summed, msg, pen, lg, mx = [sem(n) for n in ("xT", "hn", "summed", "msg", "pen", "lg", "mx")]
        LG = sb("lg", [128, G])
        attr = K.I["edge_attr_128"]

        with nc.Block() as block:
            @block.sync
            def _(sp):
                def load(at):
                    wait(sp, xT, at, late=U)
                    src = K.xs0[:, bass.ds(at.n * (R * D), R * D)] if not at.fixed() else K.xs0[:, at.n * R * D:(at.n + 1) * R * D]
                    move(sp, X[at.slot], src, loaded[at.slot])
                    move(sp, A[at.slot], rows(attr, at), loaded[at.slot])

                run(sp, EG, [(0, load)])

            @block.tensor
            def _(pe):
                def transpose(at):
                    wait_slot(pe, loaded, at, per=64)
                    wait(pe, hn, at, late=2)
                    wait(pe, summed, at, late=2)
                    for j in range(R):
                        nc.tensor.transpose(pX[at.slot % 2][:, P * j:P * j + P], X[at.slot][:, D * j:D * j + D], K.ident[0:P, 0:P])
                        t = nc.tensor.transpose(pA[at.slot % 2][:, P * j:P * j + P], A[at.slot][:, D * j:D * j + D], K.ident[0:P, 0:P])
                    t.then_inc(xT, 1)

                run(pe, EG, [(1, transpose)])

            @block.scalar
            def _(act):
                def hidden(at):
                    wait(act, xT, at)
                    wait(act, summed, at, late=2)
                    nc.scalar.activation(HN[at.slot % 2][:, :], pX[at.slot % 2][:, 0:G], ACT.Relu, bias=K.c("o0"),
                                         scale=K.c("s0")).then_inc(hn, 1)

                run(act, EG, [(1, hidden)])

            @block.vector
            def _(dve):
                def message(at):
                    i = at.slot % 2
                    wait(dve, hn, at)
                    wait(dve, msg, at, late=2)
                    nc.vector.tensor_tensor(M2[i][:, :], HN[i][:, :], pA[i][:, 0:G], ALU.add).then_inc(summed, 1)
                    wait(dve, mx, at, late=2)
                    nc.vector.tensor_scalar(PEN[i][:, :], cut(K.same, at.n, at.fixed()), 1.0, 3.0e38, ALU.subtract, ALU.mult).then_inc(pen, 1)
                    wait(dve, summed, at)
                    nc.vector.tensor_scalar(by_row(cut(QH, at.n, at.fixed())), tiles(M2[i][:, :]), 0.0, 1e-7, ALU.max, ALU.add).then_inc(msg, 1)
                    wait(dve, msg, at)
                    nc.vector.tensor_scalar(LG[i][:, :], cut(QH, at.n, at.fixed()), K.c("t"), None, ALU.mult).then_inc(lg, 1)
                    wait(dve, lg, at)
                    wait(dve, pen, at)
                    wait(dve, mx, at, late=1)
                    if at.fixed() and at.n == 0:
                        before = -3.0e38
                    else:
                        before = MX[:, at.n * G - 1:at.n * G] if at.fixed() else MX[:, bass.ds(at.n * G - 1, 1)]
                    nc.vector.tensor_tensor_scan(cut(MX, at.n, at.fixed()), PEN[i][:, :], LG[i][:, :], before,
                                                 ALU.add, ALU.max).then_inc(mx, 1)

                run(dve, EG, [(1, message)])

        def rev(ap):
            return ap[:, ::-1]

        MB, DI, EX, ME, DEN, NUM, PN, MXT = (sb(n, [128, G]) for n in ("mb", "di", "ex", "me", "den", "num", "pn", "mxt"))
        SN = sb("sn", [128, G], BF16)
        cp = sem("cp")
        mb, di, ex, me, den, num, q, q2, pn, out, inv = [sem(n) for n in ("mb", "di", "ex", "me", "den", "num", "q", "q2", "pn", "out", "inv")]

        with nc.Block() as block:
            @block.scalar
            def _(act):
                def expo(at):
                    wait(act, di, at)
                    wait(act, den, at, late=2)
                    wait(act, me, at, late=2)
                    nc.scalar.activation(EX[at.slot % 2][:, :], DI[at.slot % 2][:, :], ACT.Exp).then_inc(ex, 1)

                run(act, EG, [(0, expo)])

            @block.vector
            def _(dve):
                def maximum(at):
                    i, b = at.slot % 2, At(at.k, at.c)
                    n = backward(at)
                    wait(dve, mb, at, late=1)
                    nc.vector.tensor_scalar(PN[i][:, :], cut(K.same, n, at.fixed(), 1), 1.0, 3.0e38, ALU.subtract, ALU.mult).then_inc(pn, 1)
                    nc.vector.tensor_scalar(MXT[i][:, :], cut(MX, n, at.fixed()), 1.0, None, ALU.mult)
                    wait(dve, num, at, late=2)
                    nc.vector.tensor_scalar(SN[i][:, :], cut(K.same, n, at.fixed(), 1), 1.0, None, ALU.mult).then_inc(cp, 1)
                    wait(dve, pn, at)
                    wait(dve, cp, at)
                    wait(dve, di, at, late=2)
                    before = -3.0e38 if at.fixed() and at.n == 0 else MB[1 - i][:, 0:1]
                    nc.vector.tensor_tensor_scan(rev(MB[i]), rev(PN[i]), rev(MXT[i]), before,
                                                 ALU.add, ALU.max).then_inc(mb, 1)
                    wait(dve, mb, at)
                    wait(dve, ex, at, late=2)
                    nc.vector.scalar_tensor_tensor(out=DI[i][:, :], in0=cut(QH, n, at.fixed()), scalar=K.c("t"), in1=MB[i][:, :],
                                                   op0=ALU.mult, op1=ALU.subtract).then_inc(di, 1)

                def sums(at):
                    i = at.slot % 2
                    n = backward(at)
                    wait(dve, ex, at)
                    wait(dve, num, at, late=2)
                    nc.vector.tensor_tensor(ME[i][:, :], EX[i][:, :], cut(QH, n, at.fixed()), ALU.mult).then_inc(me, 1)
                    wait(dve, den, at, late=1)
                    wait(dve, inv, at, late=2)
                    same = rev(SN[i])
                    first = at.fixed() and at.n == 0
                    nc.vector.tensor_tensor_scan(rev(DEN[i]), same, rev(EX[i]), 0.0 if first else DEN[1 - i][:, 0:1],
                                                 ALU.mult, ALU.add).then_inc(den, 1)
                    wait(dve, me, at)
                    wait(dve, num, at, late=1)
                    wait(dve, q2, at, late=2)
                    nc.vector.tensor_tensor_scan(rev(NUM[i]), same, rev(ME[i]), 0.0 if first else NUM[1 - i][:, 0:1],
                                                 ALU.mult, ALU.add).then_inc(num, 1)
                    wait(dve, den, at)
                    nc.vector.tensor_scalar(DI2[i][:, :], DEN[i][:, :], 1e-16, None, ALU.add).then_inc(q, 1)
                    wait(dve, q, at)
                    nc.vector.reciprocal(DI2[i][:, :], DI2[i][:, :]).then_inc(inv, 1)
                    wait(dve, inv, at)
                    wait(dve, num, at)
                    nc.vector.tensor_tensor(DI2[i][:, :], DI2[i][:, :], NUM[i][:, :], ALU.mult).then_inc(q2, 1)
                    wait(dve, q2, at)
                    nc.vector.scalar_tensor_tensor(out=cut(QH, n, at.fixed()), in0=cut(K.same, n, at.fixed()), scalar=0.5,
                                                   in1=DI2[i][:, :], op0=ALU.is_lt, op1=ALU.mult).then_inc(out, 1)

                DI2 = LG
                run(dve, EG, [(0, maximum), (1, sums)])


def segment_heads(nc, K, name, QH, table, idx=None, mean=False, keep=None):
    ctx = ExitStack()
    with ctx:
        def sb(n, shape, dt=F32, k=2):
            return [ctx.enter_context(nc.sbuf_tensor(f"{name}_{n}{i}", shape, dt)) for i in range(k)]

        def sem(n):
            return K.sem(f"{name}_{n}")

        X = sb("x", [P, R, D], k=U)
        T, S, CN = sb("t", [128, G]), sb("s", [128, G]), sb("cn", [128, G])
        pX = K.ps[0:2]
        got, kept = sem_list(K, f"{name}_got"), sem_list(K, f"{name}_kept")
        xT, t, s, q, cn, inv, me = [sem(n) for n in ("xT", "t", "s", "q", "cn", "inv", "me")]
        SN, sn = sb("sn", [128, G], BF16), sem("sn")
        ones = ctx.enter_context(nc.sbuf_tensor(f"{name}_ones", [128, G], BF16))
        ones_set = sem("ones_set")
        per = 16 * R if idx is not None else 32

        with nc.Block() as block:
            if idx is not None:
                @block.gpsimd
                def _(pool):
                    def free(i):
                        if i >= U:
                            pool.wait_ge(xT, i - U + 1)
                            if keep is not None:
                                pool.wait_ge(kept[i % U], 32 * (i // U))
                    for i in range(EG):
                        free(i)
                        for r in range(R):
                            pool.indirect_dma_start(out=X[i % U][:, r, :], out_offset=None, in_=table,
                                                    in_offset=bass.IndirectOffsetOnAxis(ap=idx[:, EG - 1 - i, r:r + 1], axis=0)).then_inc(got[i % U], 16)

            @block.sync
            def _(sp):
                def back(at):
                    return backward(at) if at.fixed() else sp.snap(backward(at))

                def part(tb, at, n):
                    ap = tb[n * G:n * G + G, :] if at.fixed() else tb[bass.ds(n * G, G), :]
                    return ap.rearrange("(p r) d -> p (r d)", p=P)

                def load(at):
                    n = back(at)
                    wait(sp, xT, at, late=U)
                    move(sp, X[at.slot][:, :, :].rearrange("p r d -> p (r d)"), part(table, at, n), got[at.slot])

                def store(at):
                    n = back(at)
                    wait_slot(sp, got, at, per=per)
                    move(sp, part(keep, at, n), X[at.slot][:, :, :].rearrange("p r d -> p (r d)"), kept[at.slot])

                if idx is None:
                    run(sp, EG, [(0, load)])
                elif keep is not None:
                    run(sp, EG, [(0, store)])
                    for i in range(U):
                        sp.wait_ge(kept[i], 32 * ((EG - i + U - 1) // U))

            @block.tensor
            def _(pe):
                def transpose(at):
                    wait_slot(pe, got, at, per=per)
                    wait(pe, t, at, late=2)
                    for j in range(R):
                        last = nc.tensor.transpose(pX[at.slot % 2][:, P * j:P * j + P], X[at.slot][:, j, :], K.ident[0:P, 0:P])
                    last.then_inc(xT, 1)

                run(pe, EG, [(0, transpose)])

            @block.scalar
            def _(act):
                def order(at):
                    wait(act, xT, at)
                    wait(act, s, at, late=2)
                    nc.scalar.activation(by_row(T[at.slot % 2][:, :]), tiles(pX[at.slot % 2][:, 0:G]), ACT.Copy).then_inc(t, 1)

                run(act, EG, [(0, order)])

            @block.vector
            def _(dve):
                def sums(at):
                    i = at.slot % 2
                    n = backward(at)
                    first = at.fixed() and at.n == 0
                    wait(dve, s, at, late=1)
                    nc.vector.tensor_scalar(SN[i][:, :], cut(K.same, n, at.fixed(), 1), 1.0, None, ALU.mult).then_inc(sn, 1)
                    wait(dve, sn, at)
                    same = SN[i][:, ::-1]
                    if mean:
                        wait(dve, cn, at, late=1)
                        wait(dve, inv, at, late=2)
                        nc.vector.tensor_tensor_scan(CN[i][:, ::-1], same, ones[:, :], 0.0 if first else CN[1 - i][:, 0:1],
                                                     ALU.mult, ALU.add).then_inc(cn, 1)
                    wait(dve, t, at)
                    wait(dve, s, at, late=1)
                    wait(dve, q, at, late=2)
                    nc.vector.tensor_tensor_scan(S[i][:, ::-1], same, T[i][:, ::-1], 0.0 if first else S[1 - i][:, 0:1],
                                                 ALU.mult, ALU.add).then_inc(s, 1)
                    src = S[i]
                    if mean:
                        wait(dve, cn, at)
                        wait(dve, q, at, late=2)
                        nc.vector.reciprocal(IV[i][:, :], CN[i][:, :]).then_inc(inv, 1)
                        wait(dve, inv, at)
                        wait(dve, s, at)
                        nc.vector.tensor_tensor(IV[i][:, :], IV[i][:, :], S[i][:, :], ALU.mult).then_inc(me, 1)
                        wait(dve, me, at)
                        src = IV[i]
                    wait(dve, s, at)
                    nc.vector.scalar_tensor_tensor(out=cut(QH, n, at.fixed()), in0=cut(K.same, n, at.fixed()), scalar=0.5,
                                                   in1=src[:, :], op0=ALU.is_lt, op1=ALU.mult).then_inc(q, 1)

                IV = sb("iv", [128, G]) if mean else None
                if mean:
                    nc.vector.memset(ones[:, :], 1.0).then_inc(ones_set, 1)
                    dve.wait_ge(ones_set, 1)
                run(dve, EG, [(0, sums)])


class Spread:

    def __init__(self, nc, K, name, ctx, QH):
        self.nc, self.K, self.QH = nc, K, QH
        self.ag = [ctx.enter_context(nc.sbuf_tensor(f"{name}_ag{i}", [128, G], F32)) for i in range(2)]
        self.done = K.sem(f"{name}_spread")

    def scan(self, dve, at, used):
        i = at.slot % 2
        wait(dve, self.done, at, late=1)
        wait(dve, used, at, late=2)
        before = 0.0 if at.fixed() and at.n == 0 else self.ag[1 - i][:, G - 1:G]
        self.nc.vector.tensor_tensor_scan(self.ag[i][:, :], cut(self.K.same, at.n, at.fixed()), cut(self.QH, at.n, at.fixed()),
                                          before, ALU.mult, ALU.add).then_inc(self.done, 1)
        wait(dve, self.done, at)
        return self.ag[i]


def gin(nc, K, name, groups, base, agg=None):
    ctx = ExitStack()
    with ctx:
        def sb(n, shape, dt=F32, k=2):
            return [ctx.enter_context(nc.sbuf_tensor(f"{name}_{n}{i}", shape, dt)) for i in range(k)]

        def sem(n):
            return K.sem(f"{name}_{n}")

        X, XT, UT, VT, VM, HR = (sb("x", [P, R * D], k=U), sb("xT", [128, G]), sb("uT", [128, G]), sb("vT", [128, G]),
                                 sb("vm", [128, G]), sb("hr", [P, R * D], k=U))
        VS, ST, MK = sb("vs", [128, G], BF16), sb("st", [128, 2]), sb("mk", [128, G], I32, k=U)
        pX, pU, pV, pH = K.ps[0:2], K.ps[2:4], K.ps[4:6], K.ps[6:8]
        xin, stored = sem_list(K, f"{name}_xin"), sem_list(K, f"{name}_stored")
        xT, xs, u, us, v, vt, vm, sq, hT, hr, tot = [sem(n) for n in ("xT", "xs", "u", "us", "v", "vt", "vm", "sq", "hT", "hr", "tot")]
        spread = Spread(nc, K, name, ctx, agg) if agg is not None else None
        per = 32 if agg is not None else 48

        with nc.Block() as block:
            @block.sync
            def _(sp):
                def load(at):
                    if agg is None:
                        m = K.M[bass.ds(at.n * G, G), :] if not at.fixed() else K.M[at.n * G:at.n * G + G, :]
                        wait(sp, vm, at, late=U)
                    wait(sp, xT, at, late=U)
                    move(sp, X[at.slot], rows(K.x1, at, base), xin[at.slot])
                    if agg is None:
                        sp.dma_start(MK[at.slot][:, :], m.rearrange("n o -> o n").to_broadcast([128, G])).then_inc(xin[at.slot], 16)

                def store(at):
                    wait(sp, hr, at)
                    move(sp, rows(K.h, at, base), HR[at.slot], stored[at.slot])

                run(sp, groups, [(0, load), (3, store)])
                for i in range(U):
                    sp.wait_ge(stored[i], 32 * ((groups - i + U - 1) // U))

            @block.tensor
            def _(pe):
                def transpose_x(at):
                    wait_slot(pe, xin, at, per=per)
                    wait(pe, xs, at, late=2)
                    for j in range(R):
                        t = nc.tensor.transpose(pX[at.slot % 2][:, P * j:P * j + P], X[at.slot][:, D * j:D * j + D], K.ident[0:P, 0:P])
                    t.then_inc(xT, 1)

                def first(at):
                    wait(pe, xs, at)
                    wait(pe, us, at, late=2)
                    nc.tensor.matmul(pU[at.slot % 2][:, 0:G], K.W("w1"), XT[at.slot % 2][:, :], start=True, stop=True).then_inc(u, 1)

                def second(at):
                    wait(pe, us, at)
                    wait(pe, vt, at, late=2)
                    wait(pe, vm, at, late=2)
                    nc.tensor.matmul(pV[at.slot % 2][:, 0:G], K.W("w2"), UT[at.slot % 2][:, :], start=True, stop=True).then_inc(v, 1)

                def transpose_h(at):
                    wait(pe, vt, at)
                    wait(pe, hr, at, late=2)
                    for j in range(R):
                        t = nc.tensor.transpose(pH[at.slot % 2][0:P, D * j:D * j + D], VT[at.slot % 2][:, P * j:P * j + P], K.ident[:, :])
                    t.then_inc(hT, 1)

                run(pe, groups, [(3, transpose_h), (2, first), (1, transpose_x), (2, second)])

            @block.scalar
            def _(act):
                def copy_x(at):
                    wait(act, xT, at)
                    wait(act, u, at, late=2)
                    nc.scalar.activation(XT[at.slot % 2][:, :], pX[at.slot % 2][:, 0:G], ACT.Copy).then_inc(xs, 1)

                def relu_u(at):
                    wait(act, u, at)
                    wait(act, v, at, late=2)
                    nc.scalar.activation(UT[at.slot % 2][:, :], pU[at.slot % 2][:, 0:G], ACT.Relu, bias=K.c("L1_b1")).then_inc(us, 1)

                def copy_v(at):
                    wait(act, v, at)
                    wait(act, hT, at, late=2)
                    nc.scalar.activation(VT[at.slot % 2][:, :], pV[at.slot % 2][:, 0:G], ACT.Identity, bias=K.c("L1_b2")).then_inc(vt, 1)

                def square(at):
                    wait(act, vm, at)
                    wait(act, tot, at, late=2)
                    nc.scalar.activation(VS[at.slot % 2][:, :], VM[at.slot % 2][:, :], ACT.Square,
                                         accum_out=ST[at.slot % 2][:, 1:2]).then_inc(sq, 1)

                stages = [(2, relu_u), (2, copy_v), (3, square)]
                if agg is None:
                    stages.insert(1, (1, copy_x))
                run(act, groups, stages)

            @block.vector
            def _(dve):
                def add_agg(at):
                    a = spread.scan(dve, at, xs)
                    wait(dve, xT, at)
                    wait(dve, u, at, late=2)
                    nc.vector.tensor_tensor(tiles(XT[at.slot % 2][:, :]), tiles(pX[at.slot % 2][:, 0:G]), by_row(a[:, :]), ALU.add).then_inc(xs, 1)

                def counted(at):
                    wait(dve, vt, at)
                    wait(dve, sq, at, late=2)
                    wait(dve, tot, at, late=2)
                    if agg is None:
                        mask, limit = MK[at.slot][:, :], float(N)
                    else:
                        mask, limit = cut(K.same, at.n, at.fixed(), 1), 0.5
                    nc.vector.scalar_tensor_tensor(out=tiles(VM[at.slot % 2][:, :]), in0=by_row(mask), scalar=limit,
                                                   in1=tiles(pV[at.slot % 2][:, 0:G]), op0=ALU.is_lt, op1=ALU.mult,
                                                   accum_out=ST[at.slot % 2][:, 0:1]).then_inc(vm, 1)

                def rows_h(at):
                    wait(dve, hT, at)
                    wait_slot(dve, stored, at, per=32, late=U)
                    nc.vector.tensor_copy(HR[at.slot][:, :], pH[at.slot % 2][0:P, :]).then_inc(hr, 1)

                def total(at):
                    wait(dve, sq, at)
                    wait(dve, vm, at)
                    wait(dve, tot, at, late=1)
                    nc.vector.tensor_tensor(K.bn_sum[:, :], K.bn_sum[:, :], ST[at.slot % 2][:, :], ALU.add).then_inc(tot, 1)

                stages = [(2, counted), (3, rows_h), (3, total)]
                if agg is not None:
                    stages.insert(0, (1, add_agg))
                run(dve, groups, stages)


def bn_fold(nc, K):
    def sem(n):
        return K.sem(f"bn_{n}")

    made, sq, e, ln, pc = sem("made"), sem("sq"), sem("e"), sem("ln"), sem("pc")
    c = [K.fold[:, i:i + 1] for i in range(8)]
    n = 1.0 / N
    with nc.Block() as block:
        @block.vector
        def _(dve):
            chain = [0]

            def link(ins):
                chain[0] += 1
                ins.then_inc(made, 1)
                dve.wait_ge(made, chain[0])

            link(nc.vector.tensor_scalar(K.fold[:, 0:2], K.bn_sum[:, :], n, None, ALU.mult))
            link(nc.vector.tensor_tensor(c[2], c[0], c[0], ALU.mult))
            link(nc.vector.tensor_tensor(c[2], c[1], c[2], ALU.subtract))
            dve.wait_ge(sq, 1)
            link(nc.vector.reciprocal(c[3], c[3]))
            link(nc.vector.tensor_tensor(K.bs[:, :], c[3], K.c("gamma"), ALU.mult))
            link(nc.vector.tensor_tensor(c[4], c[0], K.c("L1_b2"), ALU.add))
            link(nc.vector.tensor_tensor(c[4], c[4], K.bs[:, :], ALU.mult))
            link(nc.vector.tensor_tensor(K.bo[:, :], K.c("beta"), c[4], ALU.subtract))
            link(nc.vector.tensor_scalar(c[5], K.c("bo1"), 0.0, LOG2, ALU.max, ALU.subtract))
            dve.wait_ge(ln, 1)
            link(nc.vector.tensor_tensor(c[6], c[5], c[6], ALU.add))
            link(nc.vector.tensor_scalar(K.spc[:, :], K.ident[:, :], 0.0, c[6], ALU.mult, ALU.add))
            dve.wait_ge(pc, 1)
            link(nc.vector.tensor_tensor(K.alone[:, :], K.ps[0][:, 0:128], K.bo2_rows[:, :], ALU.add))

        @block.scalar
        def _(act):
            act.wait_ge(made, 3)
            nc.scalar.activation(c[3], c[2], ACT.Sqrt, bias=K.eps[:, :]).then_inc(sq, 1)
            nc.scalar.activation(c[7], K.c("bo1"), ACT.Abs).then_inc(e, 1)
            act.wait_ge(e, 1)
            nc.scalar.activation(c[7], c[7], ACT.Exp, scale=-1.0).then_inc(e, 1)
            act.wait_ge(e, 2)
            nc.scalar.activation(c[6], c[7], ACT.Ln, bias=K.one[:, :]).then_inc(ln, 1)

        @block.tensor
        def _(pe):
            pe.wait_ge(made, 11)
            nc.tensor.matmul(K.ps[0][:, 0:128], K.spc[:, :], K.W("o2"), start=True, stop=True).then_inc(pc, 1)


LOG2 = float(np.log(2.0))


def gin_norm(nc, K, name, groups, x1, h, out):
    ctx = ExitStack()
    with ctx:
        def sb(n, shape, dt=F32, k=2):
            return [ctx.enter_context(nc.sbuf_tensor(f"{name}_{n}{i}", shape, dt)) for i in range(k)]

        def sem(n):
            return K.sem(f"{name}_{n}")

        X, H, X2 = sb("x", [P, R, D], k=U), sb("h", [P, R, D], k=U), sb("x2", [P, R, D], k=U)
        BT, A = sb("bT", [128, G]), sb("a", [P, R, D])
        norm = Norm(nc, K, name, ctx)
        pH, pB = K.ps[0:2], K.ps[2:4]
        xin, stored = sem_list(K, f"{name}_xin"), sem_list(K, f"{name}_stored")
        hT, bt, b, a = [sem(n) for n in ("hT", "bt", "b", "a")]

        with nc.Block() as block:
            @block.sync
            def _(sp):
                def load(at):
                    wait(sp, a, at, late=U)
                    move(sp, X[at.slot][:, :, :].rearrange("p r d -> p (r d)"), x1(at), xin[at.slot])
                    move(sp, H[at.slot][:, :, :].rearrange("p r d -> p (r d)"), h(at), xin[at.slot])

                def store(at):
                    wait(sp, norm.done, at)
                    move(sp, out(at), X2[at.slot][:, :, :].rearrange("p r d -> p (r d)"), stored[at.slot])

                run(sp, groups, [(0, load), (3, store)])
                for i in range(U):
                    sp.wait_ge(stored[i], 32 * ((groups - i + U - 1) // U))

            @block.tensor
            def _(pe):
                relu_transposes(nc, K, pe, groups, H, BT, pH, pB, xin, hT, bt, b, a)

            @block.scalar
            def _(act):
                run(act, groups, [(1, relu_bn(nc, K, act, pH, BT, hT, bt, b)), (2, norm.std_of(act))])

            @block.vector
            def _(dve):
                def residual(at):
                    wait(dve, b, at)
                    wait(dve, norm.done, at, late=2)
                    nc.vector.scalar_tensor_tensor(out=A[at.slot % 2][:, :, :], in0=X[at.slot][:, :, :], scalar=2.0,
                                                   in1=pB[at.slot % 2][0:P, :].rearrange("p (r d) -> p r d", r=R),
                                                   op0=ALU.mult, op1=ALU.add).then_inc(a, 1)

                def finish(at):
                    wait_slot(dve, stored, at, per=32, late=U)
                    norm.apply(dve, at, A[at.slot % 2], X2[at.slot])

                run(dve, groups, [(2, residual), (2, norm.stats_of(dve, A, a)), (3, finish)])


def relu_bn(nc, K, act, pH, BT, hT, bt, b):
    def stage(at):
        wait(act, hT, at)
        wait(act, b, at, late=2)
        nc.scalar.activation(BT[at.slot % 2][:, :], pH[at.slot % 2][:, 0:G], ACT.Relu, bias=K.bo[:, :], scale=K.bs[:, :]).then_inc(bt, 1)
    return stage


def relu_transposes(nc, K, pe, groups, H, BT, pH, pB, xin, hT, bt, b, a, ahead=(), more=()):
    def there(at):
        wait_slot(pe, xin, at, per=64)
        wait(pe, bt, at, late=2)
        for j in range(R):
            t = nc.tensor.transpose(pH[at.slot % 2][:, P * j:P * j + P], H[at.slot][:, j, :], K.ident[0:P, 0:P])
        t.then_inc(hT, 1)

    def back(at):
        wait(pe, bt, at)
        wait(pe, a, at, late=len(pB))
        for j in range(R):
            t = nc.tensor.transpose(pB[at.slot % len(pB)][0:P, D * j:D * j + D], BT[at.slot % 2][:, P * j:P * j + P], K.ident[:, :])
        t.then_inc(b, 1)

    run(pe, groups, [*ahead, (2, back), (1, there), *more])


def nodes_alone(nc, K, out, side=None):
    name = "al"
    ctx = ExitStack()
    with ctx:
        def sb(n, shape, dt=F32, k=2):
            return [ctx.enter_context(nc.sbuf_tensor(f"{name}_{n}{i}", shape, dt)) for i in range(k)]

        def sem(n):
            return K.sem(f"{name}_{n}")

        X, H, OUT = sb("x", [P, R, D], k=U), sb("h", [P, R, D], k=U), sb("out", [P, R, D], k=U)
        BT, A, B, X3, X3T, H3T, C = (sb("bT", [128, G]), sb("a", [P, R, D]), sb("b", [P, R, D]), sb("x3", [P, R, D], k=U),
                                     sb("x3T", [128, G]), sb("h3T", [128, G]), sb("c", [P, R, D]))
        n2, n3, n4 = Norm(nc, K, name + "2", ctx), Norm(nc, K, name + "3", ctx), Norm(nc, K, name + "4", ctx)
        pH, pB, pX, pU, pO = K.ps[0:2], K.ps[2:3], K.ps[3:5], K.ps[5:6], K.ps[6:8]
        xin, stored = sem_list(K, f"{name}_xin"), sem_list(K, f"{name}_stored")
        hT, bt, b, a, bb, xT, xt, u, ut, o, c = [sem(n) for n in ("hT", "bt", "b", "a", "bb", "xT", "xt", "u", "ut", "o", "c")]
        n2.done = bb

        with nc.Block() as block:
            if side is not None:
                block.gpsimd(side)

            @block.sync
            def _(sp):
                def load(at):
                    wait(sp, a, at, late=U)
                    move(sp, X[at.slot][:, :, :].rearrange("p r d -> p (r d)"), rows(K.x1, at), xin[at.slot])
                    move(sp, H[at.slot][:, :, :].rearrange("p r d -> p (r d)"), rows(K.h, at), xin[at.slot])

                def store(at):
                    wait(sp, n4.done, at)
                    move(sp, rows(out, at), OUT[at.slot][:, :, :].rearrange("p r d -> p (r d)"), stored[at.slot])

                run(sp, NG, [(0, load), (7, store)])
                for i in range(U):
                    sp.wait_ge(stored[i], 32 * ((NG - i + U - 1) // U))

            @block.tensor
            def _(pe):
                def transpose_x3(at):
                    wait(pe, n3.done, at)
                    wait(pe, xt, at, late=2)
                    for j in range(R):
                        t = nc.tensor.transpose(pX[at.slot % 2][:, P * j:P * j + P], X3[at.slot][:, j, :], K.ident[0:P, 0:P])
                    t.then_inc(xT, 1)

                def first(at):
                    wait(pe, xt, at)
                    wait(pe, ut, at, late=1)
                    nc.tensor.matmul(pU[0][:, 0:G], K.W("W1rT"), X3T[at.slot % 2][:, :], start=True, stop=True).then_inc(u, 1)

                def second(at):
                    wait(pe, ut, at)
                    wait(pe, c, at, late=2)
                    for j in range(R):
                        out_ = pO[at.slot % 2][0:P, D * j:D * j + D]
                        nc.tensor.matmul(out_, H3T[at.slot % 2][:, P * j:P * j + P], K.W("W2rT"), start=True, stop=False)
                        t = nc.tensor.matmul(out_, K.ones3[:, 0:P], K.bias[:, 384:512], start=False, stop=True)
                    t.then_inc(o, 1)

                relu_transposes(nc, K, pe, NG, H, BT, pH, pB, xin, hT, bt, b, a,
                                ahead=[(5, transpose_x3)], more=[(5, first), (6, second)])

            @block.scalar
            def _(act):
                def copy_x3(at):
                    wait(act, xT, at)
                    wait(act, u, at, late=2)
                    nc.scalar.activation(X3T[at.slot % 2][:, :], pX[at.slot % 2][:, 0:G], ACT.Copy).then_inc(xt, 1)

                def relu_u(at):
                    wait(act, u, at)
                    wait(act, o, at, late=2)
                    nc.scalar.activation(H3T[at.slot % 2][:, :], pU[0][:, 0:G], ACT.Relu, bias=K.c("b1l")).then_inc(ut, 1)

                run(act, NG, [(5, copy_x3), (1, relu_bn(nc, K, act, pH, BT, hT, bt, b)), (5, relu_u), (2, n2.std_of(act)),
                              (7, n4.std_of(act)), (3, n3.std_of(act))])

            @block.vector
            def _(dve):
                def residual(at):
                    wait(dve, b, at)
                    wait(dve, bb, at, late=2)
                    nc.vector.scalar_tensor_tensor(out=A[at.slot % 2][:, :, :], in0=X[at.slot][:, :, :], scalar=2.0,
                                                   in1=pB[0][0:P, :].rearrange("p (r d) -> p r d", r=R),
                                                   op0=ALU.mult, op1=ALU.add).then_inc(a, 1)

                def add_alone(at):
                    i = at.slot % 2
                    wait(dve, n2.std, at)
                    wait(dve, n3.done, at, late=2)
                    nc.vector.reciprocal(n2.sd[i][:, :], n2.sd[i][:, :]).then_inc(n2.rstd, 1)
                    wait(dve, n2.rstd, at)
                    for j in range(R):
                        t = nc.vector.scalar_tensor_tensor(out=B[i][:, j, :], in0=A[i][:, j, :], scalar=n2.sd[i][:, j:j + 1],
                                                           in1=K.alone[0:P, :], op0=ALU.mult, op1=ALU.add)
                    t.then_inc(bb, 1)

                def finish3(at):
                    wait(dve, c, at, late=U)
                    n3.apply(dve, at, B[at.slot % 2], X3[at.slot])

                def residual3(at):
                    wait(dve, o, at)
                    wait(dve, n4.done, at, late=2)
                    nc.vector.tensor_tensor(C[at.slot % 2][:, :, :], X3[at.slot][:, :, :],
                                            pO[at.slot % 2][0:P, :].rearrange("p (r d) -> p r d", r=R), ALU.add).then_inc(c, 1)

                def finish(at):
                    wait_slot(dve, stored, at, per=32, late=U)
                    n4.apply(dve, at, C[at.slot % 2], OUT[at.slot])

                run(dve, NG, [(2, residual), (2, n2.stats_of(dve, A, a)), (3, add_alone), (3, n3.stats_of(dve, B, bb)),
                              (4, finish3), (6, residual3), (6, n4.stats_of(dve, C, c)), (7, finish)])


def messages(nc, K, CR):
    ctx = ExitStack()
    with ctx:
        def sb(n, shape, dt=F32, k=2):
            return [ctx.enter_context(nc.sbuf_tensor(f"me_{n}{i}", shape, dt)) for i in range(k)]

        def sem(n):
            return K.sem(f"me_{n}")

        X, F, EW = sb("x", [P, R * D], k=U), sb("f", [P, R * RBF], k=U), sb("ew", [P, R], k=U)
        XT, FT, AB, RL, SP, WT, MT = (sb(n, [128, G]) for n in ("xT", "fT", "ab", "rl", "sp", "wT", "mT"))
        MR, SEL, SCR = sb("mr", [P, R, D]), sb("sel", [P, R, P], k=U), sb("scr", [P, R, P], BF16)
        SC, CNT, DL, DF = (sb(n, [P, R]) for n in ("sc", "cnt", "dl", "df"))
        tri = ctx.enter_context(nc.sbuf_tensor("me_tri", [P, P], F32))
        trash = ctx.enter_context(nc.sbuf_tensor("me_trash", [P, 1], F32))
        pX, pF, pH, pG, pW, pM, pS, pC = K.ps
        xin = sem_list(K, "me_xin")
        (xT, xt, fT, ft, hp, gp, ab, e1, ln, rl, sp_, wp, wt, mt, mT, mr, sc, sT, sel, cnt, dl, df, fi, cp, cr, tr) = [
            sem(n) for n in ("xT", "xt", "fT", "ft", "hp", "gp", "ab", "e1", "ln", "rl", "sp", "wp", "wt", "mt", "mT", "mr",
                             "sc", "sT", "sel", "cnt", "dl", "df", "fi", "cp", "cr", "tr")]

        with nc.Block() as block:
            @block.gpsimd
            def _(pool):
                nc.gpsimd.memset(tri[:, :], 1.0).then_inc(tr, 1)
                pool.wait_ge(tr, 1)
                nc.gpsimd.affine_select(out=tri[:, :], in_=tri[:, :], compare_op=ALU.is_gt, fill=0.0, base=0,
                                        pattern=[[-1, P]], channel_multiplier=1).then_inc(tr, 1)
                nc.gpsimd.iota(trash[:, :], pattern=[[0, 1]], base=N, channel_multiplier=1,
                               allow_small_or_imprecise_dtypes=True).then_inc(tr, 1)

            @block.sync
            def _(sp):
                def load(at):
                    f = rows(K.I["edge_attr_20"], at)
                    w = K.I["edge_weight"].rearrange("(e o) -> e o", o=1)
                    w = rows(w, at)
                    wait(sp, xT, at, late=U)
                    wait(sp, mr, at, late=U)
                    move(sp, X[at.slot], rows(K.x2d, at), xin[at.slot])
                    move(sp, F[at.slot], f, xin[at.slot])
                    sp.dma_start(EW[at.slot][:, :], w).then_inc(xin[at.slot], 16)

                run(sp, EG, [(0, load)])

            @block.tensor
            def _(pe):
                def start(at):
                    i = at.slot % 2
                    wait_slot(pe, xin, at, per=80)
                    wait(pe, ft, at, late=1)
                    for j in range(R):
                        t = nc.tensor.transpose(pF[0:RBF, P * j:P * j + P], F[at.slot][:, RBF * j:RBF * j + RBF], K.ident[0:P, 0:P])
                    t.then_inc(fT, 1)
                    wait(pe, xt, at, late=1)
                    for j in range(R):
                        t = nc.tensor.transpose(pX[:, P * j:P * j + P], X[at.slot][:, D * j:D * j + D], K.ident[0:P, 0:P])
                    t.then_inc(xT, 1)
                    wait(pe, sc, at)
                    wait(pe, sel, at, late=1)
                    for j in range(R):
                        t = nc.tensor.transpose(pS[0:P, P * j:P * j + P], SC[i][:, j:j + 1].to_broadcast([P, P]), K.ident[0:P, 0:P])
                    t.then_inc(sT, 1)

                def first(at):
                    i = at.slot % 2
                    wait(pe, ft, at)
                    wait(pe, rl, at, late=1)
                    nc.tensor.matmul(pG[:, 0:G], K.wf1[:, :], FT[i][0:RBF, :], start=True, stop=True).then_inc(gp, 1)
                    wait(pe, xt, at)
                    wait(pe, mt, at, late=1)
                    nc.tensor.matmul(pH[:, 0:G], K.W("in2f"), XT[i][:, :], start=True, stop=True).then_inc(hp, 1)

                def second(at):
                    i = at.slot % 2
                    wait(pe, sp_, at)
                    wait(pe, wt, at, late=1)
                    nc.tensor.matmul(pW[:, 0:G], K.W("f2"), SP[i][:, :], start=True, stop=True).then_inc(wp, 1)

                def third(at):
                    i = at.slot % 2
                    wait(pe, mt, at)
                    wait(pe, mr, at, late=1)
                    for j in range(R):
                        t = nc.tensor.transpose(pM[0:P, D * j:D * j + D], MT[i][:, P * j:P * j + P], K.ident[:, :])
                    t.then_inc(mT, 1)

                def combine(at):
                    i = at.slot % 2
                    wait(pe, mr, at)
                    wait(pe, sel, at)
                    wait(pe, cr, at, late=1)
                    for j in range(R):
                        t = nc.tensor.matmul(pC[0:P, D * j:D * j + D], SEL[at.slot][:, j, :], MR[i][:, j, :], start=True, stop=True)
                    t.then_inc(cp, 1)

                run(pe, EG, [(4, combine), (3, third), (2, second), (0, start), (1, first)])

            @block.scalar
            def _(act):
                def copies(at):
                    i = at.slot % 2
                    wait(act, fT, at)
                    wait(act, gp, at, late=2)
                    nc.scalar.activation(FT[i][0:RBF, :], pF[0:RBF, 0:G], ACT.Copy).then_inc(ft, 1)
                    wait(act, xT, at)
                    wait(act, hp, at, late=2)
                    nc.scalar.activation(XT[i][:, :], pX[:, 0:G], ACT.Copy).then_inc(xt, 1)

                def soft(at):
                    i = at.slot % 2
                    wait(act, gp, at)
                    wait(act, sp_, at, late=2)
                    nc.scalar.activation(AB[i][:, :], pG[:, 0:G], ACT.Abs, bias=K.c("bf1")).then_inc(ab, 1)
                    wait(act, ab, at)
                    nc.scalar.activation(AB[i][:, :], AB[i][:, :], ACT.Exp, scale=-1.0).then_inc(e1, 1)
                    wait(act, e1, at)
                    nc.scalar.activation(AB[i][:, :], AB[i][:, :], ACT.Ln, bias=K.one[:, :]).then_inc(ln, 1)

                def weights(at):
                    i = at.slot % 2
                    wait(act, wp, at)
                    wait(act, mt, at, late=2)
                    nc.scalar.activation(WT[i][:, :], pW[:, 0:G], ACT.Identity, bias=K.c("bf2")).then_inc(wt, 1)

                run(act, EG, [(2, weights), (0, copies), (1, soft)])

            @block.vector
            def _(dve):
                def column(at):
                    i = at.slot % 2
                    wait(dve, fi, at, late=2)
                    wait(dve, sT, at, late=2)
                    idx = K.src[:, at.n, :] if at.fixed() else K.src[:, bass.ds(at.n, 1), :].rearrange("p a r -> p (a r)")
                    nc.vector.tensor_scalar(SC[i][:, :], idx, 1.0, None, ALU.mult).then_inc(sc, 1)

                def soft(at):
                    i = at.slot % 2
                    wait(dve, ab, at)
                    wait(dve, sp_, at, late=2)
                    nc.vector.tensor_scalar(RL[i][:, :], pG[:, 0:G], K.c("bf1"), 0.0, ALU.add, ALU.max).then_inc(rl, 1)
                    wait(dve, rl, at)
                    wait(dve, ln, at)
                    wait(dve, wp, at, late=2)
                    nc.vector.scalar_tensor_tensor(out=SP[i][:, :], in0=RL[i][:, :], scalar=LOG2, in1=AB[i][:, :],
                                                   op0=ALU.subtract, op1=ALU.add).then_inc(sp_, 1)

                def select(at):
                    i = at.slot % 2
                    wait(dve, sT, at)
                    wait(dve, cp, at, late=U)
                    for j in range(R):
                        t = nc.vector.tensor_scalar(SEL[at.slot][:, j, :], pS[0:P, P * j:P * j + P], SC[i][:, j:j + 1], None, ALU.is_equal)
                    t.then_inc(sel, 1)
                    wait(dve, sel, at)
                    wait(dve, df, at, late=2)
                    for j in range(R):
                        t = nc.vector.scalar_tensor_tensor(out=SCR[i][:, j, :], in0=SEL[at.slot][:, j, :], scalar=1.0, in1=tri[:, :],
                                                           op0=ALU.mult, op1=ALU.mult, accum_out=CNT[i][:, j:j + 1])
                    t.then_inc(cnt, 1)
                    nc.vector.tensor_scalar(DL[i][:, :], SC[i][:, :], -1.0, trash[:, :], ALU.mult, ALU.add).then_inc(dl, 1)
                    wait(dve, dl, at)
                    wait(dve, cnt, at)
                    nc.vector.scalar_tensor_tensor(out=DF[i][:, :], in0=CNT[i][:, :], scalar=0.5, in1=DL[i][:, :],
                                                   op0=ALU.is_gt, op1=ALU.mult).then_inc(df, 1)
                    wait(dve, df, at)
                    idx = K.first[:, at.n, :] if at.fixed() else K.first[:, bass.ds(at.n, 1), :].rearrange("p a r -> p (a r)")
                    nc.vector.tensor_tensor(idx, DF[i][:, :], SC[i][:, :], ALU.add).then_inc(fi, 1)

                def product(at):
                    i = at.slot % 2
                    wait(dve, wt, at)
                    wait(dve, hp, at)
                    wait(dve, mT, at, late=2)
                    nc.vector.tensor_tensor(MT[i][:, :], WT[i][:, :], pH[:, 0:G], ALU.mult).then_inc(mt, 1)

                def weigh(at):
                    i = at.slot % 2
                    wait(dve, mT, at)
                    wait(dve, cp, at, late=2)
                    for j in range(R):
                        t = nc.vector.tensor_scalar(MR[i][:, j, :], pM[0:P, D * j:D * j + D], EW[at.slot][:, j:j + 1], None, ALU.mult)
                    t.then_inc(mr, 1)

                def keep(at):
                    wait(dve, cp, at)
                    out_ = CR[:, at.n, :] if at.fixed() else CR[:, bass.ds(at.n, 1), :].rearrange("p a n -> p (a n)")
                    nc.vector.tensor_scalar(out_, pC[0:P, :], 1.0, None, ALU.mult).then_inc(cr, 1)

                dve.wait_ge(tr, 3)
                run(dve, EG, [(4, keep), (3, weigh), (2, product), (0, column), (0, select), (1, soft)])


def schnet_update(nc, K, name, x2, y, out):
    ctx = ExitStack()
    with ctx:
        def sb(n, shape, dt=F32, k=2):
            return [ctx.enter_context(nc.sbuf_tensor(f"{name}_{n}{i}", shape, dt)) for i in range(k)]

        def sem(n):
            return K.sem(f"{name}_{n}")

        X, Y, X3 = sb("x", [P, R, D], k=U), sb("y", [P, R, D], k=U), sb("x3", [P, R, D], k=U)
        YT, AB, RL, SP = (sb(n, [128, G]) for n in ("yT", "ab", "rl", "sp"))
        A = sb("a", [P, R, D])
        norm = Norm(nc, K, name, ctx)
        pY, pG, pO = K.ps[0:2], K.ps[2:4], K.ps[4:6]
        xin, stored = sem_list(K, f"{name}_xin"), sem_list(K, f"{name}_stored")
        yT, yt, g, ab, e1, ln, rl, sp_, o, a = [sem(n) for n in ("yT", "yt", "g", "ab", "e1", "ln", "rl", "sp", "o", "a")]

        with nc.Block() as block:
            @block.sync
            def _(sp):
                def load(at):
                    wait(sp, a, at, late=U)
                    move(sp, X[at.slot][:, :, :].rearrange("p r d -> p (r d)"), rows(x2, at), xin[at.slot])
                    move(sp, Y[at.slot][:, :, :].rearrange("p r d -> p (r d)"), y(at), xin[at.slot])

                def store(at):
                    wait(sp, norm.done, at)
                    move(sp, rows(out, at), X3[at.slot][:, :, :].rearrange("p r d -> p (r d)"), stored[at.slot])

                run(sp, EG, [(0, load), (3, store)])
                for i in range(U):
                    sp.wait_ge(stored[i], 32 * ((EG - i + U - 1) // U))

            @block.tensor
            def _(pe):
                def start(at):
                    wait_slot(pe, xin, at, per=64)
                    wait(pe, yt, at, late=2)
                    for j in range(R):
                        t = nc.tensor.transpose(pY[at.slot % 2][:, P * j:P * j + P], Y[at.slot][:, j, :], K.ident[0:P, 0:P])
                    t.then_inc(yT, 1)

                def first(at):
                    wait(pe, yt, at)
                    wait(pe, rl, at, late=2)
                    nc.tensor.matmul(pG[at.slot % 2][:, 0:G], K.W("o1"), YT[at.slot % 2][:, :], start=True, stop=True).then_inc(g, 1)

                def second(at):
                    wait(pe, sp_, at)
                    wait(pe, a, at, late=2)
                    for j in range(R):
                        out_ = pO[at.slot % 2][0:P, D * j:D * j + D]
                        nc.tensor.matmul(out_, SP[at.slot % 2][:, P * j:P * j + P], K.W("o2"), start=True, stop=False)
                        t = nc.tensor.matmul(out_, K.ones3[:, 0:P], K.bias[:, 512:640], start=False, stop=True)
                    t.then_inc(o, 1)

                run(pe, EG, [(2, second), (0, start), (0, first)])

            @block.scalar
            def _(act):
                def soft(at):
                    i = at.slot % 2
                    wait(act, yT, at)
                    wait(act, g, at, late=2)
                    nc.scalar.activation(YT[i][:, :], pY[i][:, 0:G], ACT.Copy).then_inc(yt, 1)
                    wait(act, g, at)
                    wait(act, sp_, at, late=2)
                    nc.scalar.activation(AB[i][:, :], pG[i][:, 0:G], ACT.Abs, bias=K.c("bo1")).then_inc(ab, 1)
                    wait(act, ab, at)
                    nc.scalar.activation(AB[i][:, :], AB[i][:, :], ACT.Exp, scale=-1.0).then_inc(e1, 1)
                    wait(act, e1, at)
                    nc.scalar.activation(AB[i][:, :], AB[i][:, :], ACT.Ln, bias=K.one[:, :]).then_inc(ln, 1)

                run(act, EG, [(0, soft), (2, norm.std_of(act))])

            @block.vector
            def _(dve):
                def soft(at):
                    i = at.slot % 2
                    wait(dve, ab, at)
                    wait(dve, sp_, at, late=2)
                    nc.vector.tensor_scalar(RL[i][:, :], pG[i][:, 0:G], K.c("bo1"), 0.0, ALU.add, ALU.max).then_inc(rl, 1)
                    wait(dve, rl, at)
                    wait(dve, ln, at)
                    wait(dve, o, at, late=2)
                    nc.vector.scalar_tensor_tensor(out=SP[i][:, :], in0=RL[i][:, :], scalar=LOG2, in1=AB[i][:, :],
                                                   op0=ALU.subtract, op1=ALU.add).then_inc(sp_, 1)

                def residual(at):
                    wait(dve, o, at)
                    wait(dve, norm.done, at, late=2)
                    nc.vector.tensor_tensor(A[at.slot % 2][:, :, :], X[at.slot][:, :, :],
                                            pO[at.slot % 2][0:P, :].rearrange("p (r d) -> p r d", r=R), ALU.add).then_inc(a, 1)

                def finish(at):
                    wait_slot(dve, stored, at, per=32, late=U)
                    norm.apply(dve, at, A[at.slot % 2], X3[at.slot])

                run(dve, EG, [(1, soft), (2, residual), (2, norm.stats_of(dve, A, a)), (3, finish)])


def sage_hidden(nc, K, name, x3, base, agg=None):
    ctx = ExitStack()
    with ctx:
        def sb(n, shape, dt=F32, k=2):
            return [ctx.enter_context(nc.sbuf_tensor(f"{name}_{n}{i}", shape, dt)) for i in range(k)]

        def sem(n):
            return K.sem(f"{name}_{n}")

        X, HR = sb("x", [P, R * D], k=U), sb("hr", [P, R * D], k=U)
        XT, HT = sb("xT", [128, G]), sb("hT", [128, G])
        pX, pU, pH = K.ps[0:2], K.ps[2:4], K.ps[4:6]
        xin, stored = sem_list(K, f"{name}_xin"), sem_list(K, f"{name}_stored")
        xT, xt, u, ht, hT, hr = [sem(n) for n in ("xT", "xt", "u", "ht", "hT", "hr")]
        spread = Spread(nc, K, name, ctx, agg) if agg is not None else None

        with nc.Block() as block:
            @block.sync
            def _(sp):
                def load(at):
                    wait(sp, xT, at, late=U)
                    move(sp, X[at.slot], rows(x3, at), xin[at.slot])

                def store(at):
                    wait(sp, hr, at)
                    move(sp, rows(K.h3, at, base), HR[at.slot], stored[at.slot])

                run(sp, EG, [(0, load), (2, store)])
                for i in range(U):
                    sp.wait_ge(stored[i], 32 * ((EG - i + U - 1) // U))

            @block.tensor
            def _(pe):
                def start(at):
                    wait_slot(pe, xin, at, per=32)
                    wait(pe, xt, at, late=2)
                    for j in range(R):
                        t = nc.tensor.transpose(pX[at.slot % 2][:, P * j:P * j + P], X[at.slot][:, D * j:D * j + D], K.ident[0:P, 0:P])
                    t.then_inc(xT, 1)

                def first(at):
                    i = at.slot % 2
                    wait(pe, xt, at)
                    wait(pe, ht, at, late=2)
                    t = nc.tensor.matmul(pU[i][:, 0:G], K.W("W1rT"), XT[i][:, :], start=True, stop=agg is None)
                    if agg is not None:
                        wait(pe, spread.done, at)
                        t = nc.tensor.matmul(pU[i][:, 0:G], K.W("W1lT"), spread.ag[i][:, :], start=False, stop=True)
                    t.then_inc(u, 1)

                def back(at):
                    i = at.slot % 2
                    wait(pe, ht, at)
                    wait(pe, hr, at, late=2)
                    for j in range(R):
                        t = nc.tensor.transpose(pH[i][0:P, D * j:D * j + D], by_row(HT[i][:, :])[:, j, :], K.ident[:, :])
                    t.then_inc(hT, 1)

                run(pe, EG, [(2, back), (0, start), (1, first)])

            @block.scalar
            def _(act):
                def copy(at):
                    i = at.slot % 2
                    wait(act, xT, at)
                    wait(act, u, at, late=2)
                    nc.scalar.activation(by_row(XT[i][:, :]), tiles(pX[i][:, 0:G]), ACT.Copy).then_inc(xt, 1)

                def relu(at):
                    i = at.slot % 2
                    wait(act, u, at)
                    wait(act, hT, at, late=2)
                    nc.scalar.activation(HT[i][:, :], pU[i][:, 0:G], ACT.Relu, bias=K.c("b1l")).then_inc(ht, 1)

                run(act, EG, [(0, copy), (1, relu)])

            @block.vector
            def _(dve):
                def aggregate(at):
                    spread.scan(dve, at, u)

                def back(at):
                    wait(dve, hT, at)
                    wait_slot(dve, stored, at, per=32, late=U)
                    nc.vector.tensor_copy(HR[at.slot][:, :], pH[at.slot % 2][0:P, :]).then_inc(hr, 1)

                run(dve, EG, ([(1, aggregate)] if agg is not None else []) + [(2, back)])


def sage_out(nc, K, name, x3, base, out, idx, agg=None):
    ctx = ExitStack()
    with ctx:
        def sb(n, shape, dt=F32, k=2):
            return [ctx.enter_context(nc.sbuf_tensor(f"{name}_{n}{i}", shape, dt)) for i in range(k)]

        def sem(n):
            return K.sem(f"{name}_{n}")

        X, H, OUT = sb("x", [P, R, D], k=U), sb("h", [P, R, D], k=U), sb("out", [P, R, D], k=U)
        HT, A = sb("hT", [128, G]), sb("a", [P, R, D])
        norm = Norm(nc, K, name, ctx)
        pH, pO = K.ps[0:2], K.ps[2:4]
        xin, sent = sem_list(K, f"{name}_xin"), sem_list(K, f"{name}_sent")
        hT, ht, o, a = [sem(n) for n in ("hT", "ht", "o", "a")]
        spread = Spread(nc, K, name, ctx, agg) if agg is not None else None

        with nc.Block() as block:
            @block.gpsimd
            def _(pool):
                for i in range(EG):
                    pool.wait_ge(norm.done, i + 1)
                    for r in range(R):
                        pool.indirect_dma_start(out=out, out_offset=bass.IndirectOffsetOnAxis(ap=idx[:, i, r:r + 1], axis=0),
                                                in_=OUT[i % U][:, r, :], in_offset=None, bounds_check=N - 1,
                                                oob_is_err=False).then_inc(sent[i % U], 16)
                for i in range(U):
                    pool.wait_ge(sent[i], 16 * R * ((EG - i + U - 1) // U))

            @block.sync
            def _(sp):
                def load(at):
                    wait(sp, a, at, late=U)
                    move(sp, X[at.slot][:, :, :].rearrange("p r d -> p (r d)"), rows(x3, at), xin[at.slot])
                    move(sp, H[at.slot][:, :, :].rearrange("p r d -> p (r d)"), rows(K.h3, at, base), xin[at.slot])

                run(sp, EG, [(0, load)])

            @block.tensor
            def _(pe):
                def start(at):
                    wait_slot(pe, xin, at, per=64)
                    wait(pe, ht, at, late=2)
                    for j in range(R):
                        t = nc.tensor.transpose(pH[at.slot % 2][:, P * j:P * j + P], H[at.slot][:, j, :], K.ident[0:P, 0:P])
                    t.then_inc(hT, 1)

                def product(at):
                    i = at.slot % 2
                    wait(pe, ht, at)
                    wait(pe, a, at, late=2)
                    if agg is not None:
                        wait(pe, spread.done, at)
                    for j in range(R):
                        out_ = pO[i][0:P, D * j:D * j + D]
                        nc.tensor.matmul(out_, HT[i][:, P * j:P * j + P], K.W("W2rT"), start=True, stop=False)
                        if agg is not None:
                            nc.tensor.matmul(out_, by_row(spread.ag[i][:, :])[:, j, :], K.W("W2lT"), start=False, stop=False)
                        t = nc.tensor.matmul(out_, K.ones3[:, 0:P], K.bias[:, 384:512], start=False, stop=True)
                    t.then_inc(o, 1)

                run(pe, EG, [(0, start), (1, product)])

            @block.scalar
            def _(act):
                def copy(at):
                    i = at.slot % 2
                    wait(act, hT, at)
                    wait(act, o, at, late=2)
                    nc.scalar.activation(HT[i][:, :], pH[i][:, 0:G], ACT.Copy).then_inc(ht, 1)

                run(act, EG, [(0, copy), (1, norm.std_of(act))])

            @block.vector
            def _(dve):
                def aggregate(at):
                    spread.scan(dve, at, o)

                def residual(at):
                    wait(dve, o, at)
                    wait(dve, norm.done, at, late=2)
                    nc.vector.tensor_tensor(A[at.slot % 2][:, :, :], X[at.slot][:, :, :],
                                            pO[at.slot % 2][0:P, :].rearrange("p (r d) -> p r d", r=R), ALU.add).then_inc(a, 1)

                def finish(at):
                    wait_slot(dve, sent, at, per=16 * R, late=U)
                    norm.apply(dve, at, A[at.slot % 2], OUT[at.slot])

                run(dve, EG, ([(1, aggregate)] if agg is not None else []) +
                    [(1, residual), (1, norm.stats_of(dve, A, a)), (2, finish)])


def h3_rows(nc, K):
    a, b = K.sem("h3_a"), K.sem("h3_b")
    with ExitStack() as ctx:
        inside, diff = [ctx.enter_context(nc.sbuf_tensor(n, [P, EG, R], F32)) for n in ("in_d", "h3_diff")]
        with nc.Block() as block:
            @block.vector
            def _(dve):
                nc.vector.tensor_tensor(diff[:, :, :], K.from_[:, :, :], K.slot[:, :, :], ALU.subtract).then_inc(a, 1)
                nc.vector.tensor_scalar(inside[:, :, :], K.from_[:, :, :], N - 0.5, None, ALU.is_gt).then_inc(a, 1)
                dve.wait_ge(a, 2)
                nc.vector.scalar_tensor_tensor(out=diff[:, :, :], in0=diff[:, :, :], scalar=float(E), in1=inside[:, :, :],
                                               op0=ALU.add, op1=ALU.mult).then_inc(a, 1)
                dve.wait_ge(a, 3)
                nc.vector.scalar_tensor_tensor(out=K.of_h3[:, :, :], in0=K.slot[:, :, :], scalar=float(N), in1=diff[:, :, :],
                                               op0=ALU.subtract, op1=ALU.add).then_inc(b, 1)
                nc.vector.tensor_tensor(inside[:, :, :], K.to_s[:, :, :], K.slot[:, :, :], ALU.not_equal).then_inc(b, 1)
                dve.wait_ge(b, 2)
                nc.vector.scalar_tensor_tensor(out=K.to_s[:, :, :], in0=inside[:, :, :], scalar=float(NOWHERE), in1=K.from_[:, :, :],
                                               op0=ALU.mult, op1=ALU.add).then_inc(b, 1)
                dve.wait_ge(b, 3)


def clear_sums(nc, K):
    s = K.sem("sums_clear")
    with nc.Block() as block:
        @block.vector
        def _(dve):
            nc.vector.memset(K.bn_sum[:, :], 0.0).then_inc(s, 1)
            dve.wait_ge(s, 1)


def debug(nc, K, table, out):
    done = K.sem("dbg")
    B = K.ctx.enter_context(nc.sbuf_tensor("dbgb", [P, EG, R, D], F32))
    d1 = K.sem("dbg1")
    d2 = K.sem("dbg2")
    with nc.Block() as block:
        @block.gpsimd
        def _(pool):
            pool.dma_start(out.rearrange("(p a) d -> p a d",p=P), table[0:N, :].rearrange("(p a) d -> p a d",p=P)).then_inc(done, 16)
            pool.dma_start(B[:, :, :, :].rearrange("p g r d -> p g (r d)"), table[N:N + E, :].rearrange("(g p r) d -> p g (r d)", p=P, r=R)).then_inc(d1, 16)
            pool.wait_ge(done, 16)
            pool.wait_ge(d1, 16)
            scatter_rows(nc, pool, out, K.to_d, lambda g, r: B[:, g, r, :], d2, N - 1)
            pool.wait_ge(d2, 16 * EG * R)


def program(nc, I, out):
    K = Kit(nc)
    K.I = I
    K.ctx = ExitStack()
    with K.ctx:
        K.ps = [K.ctx.enter_context(nc.psum_tensor(f"bank{i}", [128, 512], F32)) for i in range(8)]
        K.dst_pad = nc.dram_tensor("dst_pad", [E + 2, 1], I32).ap()
        K.M = nc.dram_tensor("row_of", [N, 1], I32).ap()
        K.owner = nc.dram_tensor("owner", [N + P, 1], I32).ap()
        K.acc = nc.dram_tensor("acc", [N + P, D], F32).ap()
        K.x1 = nc.dram_tensor("x1", [N + E, D], F32).ap()
        K.xs0 = nc.dram_tensor("x_of_src", [P, EG * R * D], F32).ap()
        K.h = nc.dram_tensor("h", [N + E, D], F32).ap()
        K.xs1, K.hs, K.x2d, K.x2s, K.ys, K.yd, K.x3s, K.x3d = [nc.dram_tensor(n, [E, D], F32).ap() for n in
            ("x1_of_src", "h_of_src", "x2_of_dst", "x2_of_src", "y_of_src", "y_of_dst", "x3_of_src", "x3_of_dst")]
        K.h3 = nc.dram_tensor("h3", [2 * E, D], F32).ap()
        K.xd0 = nc.dram_tensor("x_of_dst", [P, EG * R * D], F32).ap()
        with ExitStack() as ctx:
            setup(nc, K, I, ctx)
            K.end_phase()

        def sem(n):
            return K.sem(n)

        def by_edge(table):
            return lambda at: (table[:, at.n * (R * D):(at.n + 1) * (R * D)] if at.fixed() else
                               table[:, bass.ds(at.n * (R * D), R * D)])

        map_set, map_got, xd_got, xs_got, x_kept = [sem(n) for n in ("map_set", "map_got", "xd_got", "xs_got", "x_kept")]
        with ExitStack() as ctx:
            XD = ctx.enter_context(nc.sbuf_tensor("x_dst", [P, EG, R, D], F32))
            XS = ctx.enter_context(nc.sbuf_tensor("x_src", [P, EG, R, D], F32))

            def side(pool):
                gather_rows(nc, pool, lambda g, r: XD[:, g, r, :], I["x"], K.dst, lambda g: xd_got)
                pool.wait_ge(xd_got, 16 * EG * R)
                pool.dma_start(K.xd0, XD[:, :, :, :].rearrange("p g r d -> p (g r d)"), max_dma_last_dim=2048).then_inc(x_kept, 16)
                gather_rows(nc, pool, lambda g, r: XS[:, g, r, :], I["x"], K.src, lambda g: xs_got)
                scatter_rows(nc, pool, K.M, K.to_d, lambda g, r: K.slot[:, g, r:r + 1], map_set, N - 1)
                pool.wait_ge(xs_got, 16 * EG * R)
                pool.dma_start(K.xs0, XS[:, :, :, :].rearrange("p g r d -> p (g r d)"), max_dma_last_dim=2048).then_inc(x_kept, 16)
                pool.wait_ge(map_set, 16 * EG * R)
                gather_rows(nc, pool, lambda g, r: K.from_[:, g, r:r + 1], K.M, K.src, lambda g: map_got)
                pool.wait_ge(map_got, 16 * EG * R)
                pool.wait_ge(x_kept, 32)

            gen_dense(nc, K, "gen_n", NG, lambda at: rows(I["x"], at), K.x1, 0, None, side=side, clear=K.acc)
            K.end_phase()
        with ExitStack() as ctx:
            QH = ctx.enter_context(nc.sbuf_tensor("gen_heads", [128, E], F32))
            with ExitStack() as ctx2:
                MX = ctx2.enter_context(nc.sbuf_tensor("gen_max", [128, E], F32))
                softmax_heads(nc, K, QH, MX)
                K.end_phase()
            gen_dense(nc, K, "gen_d", EG, by_edge(K.xd0), K.x1, N, QH)
            K.end_phase()
        with ExitStack() as ctx:
            QH = ctx.enter_context(nc.sbuf_tensor("gin_heads", [128, E], F32))
            segment_heads(nc, K, "a1", QH, K.x1, idx=K.from_, keep=K.xs1)
            K.end_phase()
            clear_sums(nc, K)
            K.end_phase()
            gin(nc, K, "gin_d", EG, N, agg=QH)
            K.end_phase()
        gin(nc, K, "gin_n", NG, 0)
        K.end_phase()
        bn_fold(nc, K)
        K.end_phase()
        gin_norm(nc, K, "x2d", EG, lambda at: rows(K.x1, at, N), lambda at: rows(K.h, at, N), lambda at: rows(K.x2d, at))
        K.end_phase()
        big = ExitStack()
        CR = big.enter_context(nc.sbuf_tensor("combined", [P, EG, R * D], F32))
        messages(nc, K, CR)
        K.end_phase()
        added, owned, got_, kept_, owner_got = [sem(n) for n in ("added", "owned", "y_got", "y_kept", "owner_got")]

        def accumulate(pool):
            for i in range(EG * R):
                if i:
                    pool.wait_ge(added, 16 * i)
                pool.indirect_dma_start(out=K.acc, out_offset=bass.IndirectOffsetOnAxis(ap=K.first[:, i // R, i % R:i % R + 1], axis=0),
                                        in_=CR[:, i // R, i % R * D:i % R * D + D], in_offset=None, compute_op=ALU.add).then_inc(added, 16)
                if i:
                    pool.wait_ge(owned, 16 * i)
                pool.indirect_dma_start(out=K.owner, out_offset=bass.IndirectOffsetOnAxis(ap=K.first[:, i // R, i % R:i % R + 1], axis=0),
                                        in_=K.slot[:, i // R, i % R:i % R + 1], in_offset=None).then_inc(owned, 16)
            pool.wait_ge(owned, 16 * EG * R)
            gather_rows(nc, pool, lambda g, r: K.to_s[:, g, r:r + 1], K.owner, K.src, lambda g: owner_got)
            pool.wait_ge(owner_got, 16 * EG * R)
            pool.wait_ge(added, 16 * EG * R)
            for i, (table, idx, keep) in enumerate([(K.h, K.from_, K.hs), (K.acc, K.src, K.ys), (K.acc, K.dst, K.yd)]):
                gather_rows(nc, pool, lambda g, r: CR[:, g, r * D:r * D + D], table, idx, lambda g: got_)
                pool.wait_ge(got_, 16 * EG * R * (i + 1))
                pool.dma_start(keep.rearrange("(g p r) d -> p g (r d)", p=P, r=R), CR[:, :, :]).then_inc(kept_, 16)
                pool.wait_ge(kept_, 16 * (i + 1))

        nodes_alone(nc, K, out, side=accumulate)
        K.end_phase()
        big.close()
        gin_norm(nc, K, "x2s", EG, lambda at: rows(K.xs1, at), lambda at: rows(K.hs, at), lambda at: rows(K.x2s, at))
        K.end_phase()
        schnet_update(nc, K, "ups", K.x2s, lambda at: rows(K.ys, at), K.x3s)
        K.end_phase()
        schnet_update(nc, K, "upd", K.x2d, lambda at: rows(K.yd, at), K.x3d)
        K.end_phase()
        sage_hidden(nc, K, "shs", K.x3s, 0)
        K.end_phase()
        with ExitStack() as ctx:
            QH = ctx.enter_context(nc.sbuf_tensor("sage_heads", [128, E], F32))
            segment_heads(nc, K, "a3", QH, K.x3s, mean=True)
            K.end_phase()
            sage_hidden(nc, K, "shd", K.x3d, E, agg=QH)
            K.end_phase()
            h3_rows(nc, K)
            K.end_phase()
            segment_heads(nc, K, "a4", QH, K.h3, idx=K.of_h3, mean=True)
            K.end_phase()
            sage_out(nc, K, "sod", K.x3d, E, out, K.to_d, agg=QH)
            K.end_phase()
        sage_out(nc, K, "sos", K.x3s, 0, out, K.to_s)
        K.end_phase()


_INS = ['x', 'src', 'dst', 'edge_attr_128', 'edge_attr_20', 'edge_weight', 'L0_gnn_bn_weight', 'L0_gnn_bn_bias',
        'L0_gnn_bn_mean', 'L0_gnn_bn_var', 'L0_gnn_t', 'L0_gnn_W1', 'L0_gnn_b1', 'L0_gnn_ln_weight', 'L0_gnn_ln_bias',
        'L0_gnn_W2', 'L0_gnn_b2', 'L1_gnn_w1', 'L1_gnn_b1', 'L1_gnn_w2', 'L1_gnn_b2', 'L1_gnn_gamma', 'L1_gnn_beta',
        'L2_gnn_W_in2f', 'L2_gnn_W_f1', 'L2_gnn_b_f1', 'L2_gnn_W_f2', 'L2_gnn_b_f2', 'L2_gnn_W_o1', 'L2_gnn_b_o1',
        'L2_gnn_W_o2', 'L2_gnn_b_o2', 'L3_gnn_W1l', 'L3_gnn_b1l', 'L3_gnn_W1r', 'L3_gnn_W2l', 'L3_gnn_b2l', 'L3_gnn_W2r']


def kernel(**inputs):
    import numpy as _np
    import concourse.bacc as _bacc
    from concourse import mybir as _mybir
    from concourse.bass_utils import run_bass_kernel_spmd as _run

    nc = _bacc.Bacc("TRN2", target_bir_lowering=False, num_devices=1)
    arrays, aps = {}, {}
    for name in _INS:
        a = _np.ascontiguousarray(inputs[name])
        if a.ndim == 0:
            a = a.reshape(1)
        arrays[f"in_{name}"] = a
        aps[name] = nc.dram_tensor(f"in_{name}", a.shape, _mybir.dt.from_np(a.dtype), kind="ExternalInput").ap()
    out = nc.dram_tensor("out", (50000, 128), _mybir.dt.float32, kind="ExternalOutput").ap()
    program(nc, aps, out)
    r = _run(nc, [arrays], core_ids=[0])
    return r.results[0]["out"]
```
